# Optimizing a Trainium2 kernel written in Bass

```python
import numpy as np
import jax
import jax.numpy as jnp

def _softmax(x, axis=-1):
    return jax.nn.softmax(x, axis=axis)

def _gelu(x):
    return jax.nn.gelu(x, approximate=True)

def _silu(x):
    return jax.nn.silu(x)

def _sigmoid(x):
    return jax.nn.sigmoid(x)

def _layernorm(x, axis=-1, eps=1e-05):
    m = jnp.mean(x, axis=axis, keepdims=True)
    v = jnp.var(x, axis=axis, keepdims=True)
    return (x - m) / jnp.sqrt(v + eps)

def _scatter_add(tgt, idx, src, axis=0):
    return tgt.at[idx].add(src)

def _segment_sum(src, seg, n):
    return jax.ops.segment_sum(src, seg, n)
kernel_name = 'mk_gnn_resnorm_d1_gnn_r8_01353a'

def setup_inputs(seed: int=0):
    np.random.seed(seed)
    _w = jnp.asarray

    def _rec_inputs():
        import jax
        import jax.numpy as jnp
        _gk = jax.random.key(seed)
        x = -0.000202 + 1 * jax.random.normal(jax.random.fold_in(_gk, 1), (12500, 128), jnp.float32)
        _s = jax.random.randint(jax.random.fold_in(_gk, 2), (100000,), 0, 12500, jnp.int32)
        _d = jax.random.randint(jax.random.fold_in(_gk, 3), (100000,), 0, 12500, jnp.int32)
        _loop = jnp.arange(12500, dtype=jnp.int32)
        src = jnp.concatenate([_s, _d, _loop])
        dst = jnp.concatenate([_d, _s, _loop])
        _o = jnp.argsort(dst, stable=True)
        src = src[_o]
        dst = dst[_o]
        edge_attr3_1x20 = jax.random.uniform(jax.random.fold_in(_gk, 11), (212500, 1, 20), jnp.float32, 0.0, 1)
        edge_weight1 = jax.random.uniform(jax.random.fold_in(_gk, 13), (212500, 1), jnp.float32, 0.0, 0.999999)
        return (x, src, dst, edge_attr3_1x20, edge_weight1)
    x, src, dst, edge_attr3_1x20, edge_weight1 = _rec_inputs()

    def _L0_gnn_setup():
        import jax, jax.numpy as jnp
        import numpy as np
        N_ATOMS = 6250
        N_PAIRS = 75000
        D_FEAT = 128
        D_FILT = 128
        N_RBF = 20

        def ssp(x):
            return jax.nn.softplus(x) - jnp.log(2.0).astype(x.dtype)
        key = jax.random.key(seed)
        ks = jax.random.split(key, 12)
        inp = {'x': jax.random.normal(ks[0], (N_ATOMS, D_FEAT), dtype=jnp.float32), 'pairlist': jax.random.randint(ks[1], (2, N_PAIRS), 0, N_ATOMS, dtype=jnp.int64), 'f_ij': jax.random.uniform(ks[2], (N_PAIRS, 1, N_RBF), dtype=jnp.float32), 'f_ij_cutoff': jax.random.uniform(ks[3], (N_PAIRS, 1), dtype=jnp.float32), 'W_in': jax.random.normal(ks[4], (D_FEAT, D_FILT), dtype=jnp.float32) * 0.05, 'W_f1': jax.random.normal(ks[5], (N_RBF, D_FILT), dtype=jnp.float32) * 0.05, 'b_f1': jnp.zeros((D_FILT,), dtype=jnp.float32), 'W_f2': jax.random.normal(ks[6], (D_FILT, D_FILT), dtype=jnp.float32) * 0.05, 'b_f2': jnp.zeros((D_FILT,), dtype=jnp.float32), 'W_o1': jax.random.normal(ks[7], (D_FILT, D_FEAT), dtype=jnp.float32) * 0.05, 'b_o1': jnp.zeros((D_FEAT,), dtype=jnp.float32), 'W_o2': jax.random.normal(ks[8], (D_FEAT, D_FEAT), dtype=jnp.float32) * 0.05, 'b_o2': jnp.zeros((D_FEAT,), dtype=jnp.float32)}
        return inp
    _L0_gnn_all = _L0_gnn_setup()
    _L0_gnn_in = {k: v for k, v in _L0_gnn_all.items() if k in ('W_in', 'W_f1', 'b_f1', 'W_f2', 'b_f2', 'W_o1', 'b_o1', 'W_o2', 'b_o2')}
    del _L0_gnn_all
    return {'x': x, 'src': src, 'dst': dst, 'edge_attr3_1x20': edge_attr3_1x20, 'edge_weight1': edge_weight1, 'L0_gnn_W_in': _L0_gnn_in['W_in'], 'L0_gnn_W_f1': _L0_gnn_in['W_f1'], 'L0_gnn_b_f1': _L0_gnn_in['b_f1'], 'L0_gnn_W_f2': _L0_gnn_in['W_f2'], 'L0_gnn_b_f2': _L0_gnn_in['b_f2'], 'L0_gnn_W_o1': _L0_gnn_in['W_o1'], 'L0_gnn_b_o1': _L0_gnn_in['b_o1'], 'L0_gnn_W_o2': _L0_gnn_in['W_o2'], 'L0_gnn_b_o2': _L0_gnn_in['b_o2']}

def reference(x, src, dst, edge_attr3_1x20, edge_weight1, L0_gnn_W_in, L0_gnn_W_f1, L0_gnn_b_f1, L0_gnn_W_f2, L0_gnn_b_f2, L0_gnn_W_o1, L0_gnn_b_o1, L0_gnn_W_o2, L0_gnn_b_o2):
    import jax
    import jax.numpy as jnp

    def _L0_gnn_ref(x, pairlist, f_ij, f_ij_cutoff, W_in, W_f1, b_f1, W_f2, b_f2, W_o1, b_o1, W_o2, b_o2):
        import jax, jax.numpy as jnp
        import numpy as np
        N_ATOMS = 6250
        N_PAIRS = 75000
        D_FEAT = 128
        D_FILT = 128
        N_RBF = 20

        def ssp(x):
            return jax.nn.softplus(x) - jnp.log(2.0).astype(x.dtype)
        n_atoms = x.shape[0]
        h = x @ W_in
        Wij = ssp(f_ij[:, 0, :] @ W_f1 + b_f1) @ W_f2 + b_f2
        idx_i = pairlist[0]
        idx_j = pairlist[1]
        x_ij = h[idx_j] * Wij * f_ij_cutoff
        agg = jax.ops.segment_sum(x_ij, idx_i, num_segments=n_atoms)
        out = ssp(agg @ W_o1 + b_o1) @ W_o2 + b_o2
        return out
    edge_index = jnp.stack([src, dst])
    x = _layernorm(x + _L0_gnn_ref(x, edge_index, edge_attr3_1x20, edge_weight1, L0_gnn_W_in, L0_gnn_W_f1, L0_gnn_b_f1, L0_gnn_W_f2, L0_gnn_b_f2, L0_gnn_W_o1, L0_gnn_b_o1, L0_gnn_W_o2, L0_gnn_b_o2), axis=-1)
    return x

_drawn_inputs = setup_inputs


def setup_inputs(seed=0):
    import zlib

    import numpy as np

    out = dict(_drawn_inputs(seed))
    spreads = {'L0_gnn_b_f1': (0.0, 0.8),
     'L0_gnn_b_f2': (0.0, 0.975),
     'L0_gnn_b_o1': (0.0, 2.0),
     'L0_gnn_b_o2': (0.0, 0.8)}
    factors = {'edge_attr3_1x20': 8.0, 'edge_weight1': 4.033, 'L0_gnn_W_f1': 6.949, 'L0_gnn_W_f2': 5.469}
    for name, (base, spread) in spreads.items():
        noise = np.random.default_rng([zlib.crc32(name.encode()), seed]).standard_normal(out[name].shape)
        drawn = base * np.exp(spread * noise) if base else spread * noise
        out[name] = jnp.asarray(drawn.astype(out[name].dtype))
    for name, factor in factors.items():
        out[name] = (out[name] * factor).astype(out[name].dtype)
    return out
```

```python
import numpy as np
import concourse.bass as bass
from concourse import mybir
from contextlib import ExitStack

P = 128
ATOMS, FEAT, EDGES, RBF = 12500, 128, 212500, 20
TILES_PER_GROUP = 4
GROUP = TILES_PER_GROUP * P
SECTION = 2 * GROUP
SECTIONS = -(-EDGES // SECTION)
GROUPS = 2 * SECTIONS
TILES = GROUPS * TILES_PER_GROUP
EDGE_ROWS = SECTIONS * SECTION
ROUNDS = SECTIONS // 2
BATCH = 4 * P
BATCHES = -(-ATOMS // BATCH)
ROWS = BATCHES * BATCH
SPARE = ROWS - 2 * P
CHAINS = TILES_PER_GROUP
PARTS = 3
SLOTS = 3
EPS = 1e-5
assert SPARE >= ATOMS and SECTIONS % 2 == 0 and BATCHES % 2 == 1


def gnn_program(nc, x_rows, x_cols, src_row, dst_row, src_col, dst_col, cut_col, rbf_t,
                w_in, w_f1, b_f1, w_f2, b_f2, w_o1, b_o1, w_o2, b_o2, lane, eye, out):
    f32, bf16, i16, i32, u32 = (mybir.dt.float32, mybir.dt.bfloat16, mybir.dt.int16,
                                mybir.dt.int32, mybir.dt.uint32)
    ALU, ACT, AX = mybir.AluOpType, mybir.ActivationFunctionType, mybir.AxisListType
    ds = bass.ds
    ctx = ExitStack()
    with ctx:
        def sb(name, shape, dt):
            return ctx.enter_context(nc.sbuf_tensor(name, shape, dt))

        def sem(name):
            return ctx.enter_context(nc.semaphore(name))

        def sems(name, n):
            return [sem(f"{name}{k}") for k in range(n)]

        h_parts = nc.dram_tensor("h_parts", [ROWS, PARTS * FEAT], bf16).ap()
        src16 = nc.dram_tensor("src16", [SECTIONS, SECTION], i16).ap()
        dst16 = nc.dram_tensor("dst16", [SECTIONS, SECTION], i16).ap()
        base_dram = nc.dram_tensor("base_dram", [1, SECTIONS], f32).ap()
        span_dram = nc.dram_tensor("span_dram", [1, SECTIONS], f32).ap()
        accum = [nc.dram_tensor(f"accum{q}", [ROWS, FEAT], f32).ap() for q in range(CHAINS)]

        w_in_sb = sb("w_in_sb", [P, FEAT], f32)
        w_f1_sb = sb("w_f1_sb", [RBF + 1, FEAT], f32)
        w_f2_sb = sb("w_f2_sb", [P, FEAT], f32)
        w_o1_sb = sb("w_o1_sb", [P, FEAT], f32)
        w_o2_sb = sb("w_o2_sb", [P, FEAT], f32)
        eye_sb = sb("eye_sb", [P, P], f32)
        eye16 = sb("eye16", [P, P], bf16)
        lane_sb = sb("lane_sb", [P, 4], f32)
        ones3 = sb("ones3", [PARTS, GROUP], bf16)
        bias_row = sb("bias_row", [1, 3, GROUP], f32)
        bias_rest = sb("bias_rest", [1, 3, GROUP], f32)
        bias_part = sb("bias_part", [1, PARTS, 3 * GROUP], bf16)
        bias3 = sb("bias3", [PARTS, 3, GROUP], bf16)
        zero_rows = sb("zero_rows", [P, 20, FEAT], f32)
        cut_sb = sb("cut_sb", [P, TILES], f32)
        src_raw = sb("src_raw", [P, TILES], i32)
        src_f = sb("src_f", [P, TILES], f32)
        spare_gap = sb("spare_gap", [P, TILES], f32)
        dst_idx = sb("dst_idx", [P, TILES], i32)
        base_lane = sb("base_lane", [P, SECTIONS], f32)
        base_reg = sb("base_reg", [1, SECTIONS], i32)
        span_row = sb("span_row", [1, SECTIONS], f32)
        span_max = sb("span_max", [1, 1], f32)
        wide_flag = sb("wide_flag", [1, 1], i32)
        HALF = SECTIONS // 2
        row32 = sb("row32", [HALF, 2, 2 * SECTION], i32)
        row16 = sb("row16", [HALF, 2, 2 * SECTION], i16)
        base_f = sb("base_f", [HALF, 2], f32)
        top_f = sb("top_f", [HALF, 2], f32)
        span_f = sb("span_f", [HALF, 2], f32)

        rbf_in = sb("rbf_in", [RBF + 1, 2, SECTION], f32)
        src_rep = sb("src_rep", [P, 2, SECTION], i16)
        dst_rep = sb("dst_rep", [P, 2, SECTION], i16)
        h_win = sb("h_win", [P, 2, PARTS, FEAT], bf16)
        pick = sb("pick", [P, 2, GROUP], bf16)
        same = sb("same", [P, 2, GROUP], f32)
        az = sb("az", [P, 2, GROUP], f32)
        ez = sb("ez", [P, 2, GROUP], f32)
        yz = sb("yz", [P, 2, GROUP], f32)
        act1 = sb("act1", [P, 2, GROUP], f32)
        h_cut = sb("h_cut", [P, 2, TILES_PER_GROUP, FEAT], f32)
        msg = sb("msg", [P, 2, TILES_PER_GROUP, FEAT + 1], f32)
        merged = sb("merged", [P, 2 * TILES_PER_GROUP, FEAT], f32)
        gap = sb("gap", [P, 4, TILES_PER_GROUP], f32)
        row_idx = sb("row_idx", [P, 4, TILES_PER_GROUP], i32)
        gath_idx = sb("gath_idx", [P, 2, TILES_PER_GROUP], i32)
        gath = sb("gath", [P, 2, TILES_PER_GROUP, PARTS * FEAT], bf16)

        x_in = sb("x_in", [P, 2, BATCH], f32)
        h_out = sb("h_out", [P, 2, 4, PARTS, FEAT], bf16)
        h_rest = sb("h_rest", [P, 2, 4, FEAT], f32)
        acc_in = sb("acc_in", [P, 2, CHAINS, 4 * FEAT], f32)
        acc_half = sb("acc_half", [P, 2, 2, 4 * FEAT], f32)
        agg = sb("agg", [P, 2, 4, FEAT], f32)
        agg_t = sb("agg_t", [P, 2, BATCH], f32)
        res = sb("res", [P, 2, 4, FEAT], f32)
        stats = sb("stats", [P, 2, 4, 6], f32)
        mean_var = sb("mean_var", [P, 2, 4, 2], f32)
        rstd = sb("rstd", [P, 2, 5, 4], f32)
        y_out = h_rest
        eps_sb = sb("eps_sb", [P, 1], f32)
        half_sb = sb("half_sb", [P, 1], f32)

        ps_z = ctx.enter_context(nc.psum_tensor("ps_z", [P, 2, GROUP], f32))
        ps_w = ctx.enter_context(nc.psum_tensor("ps_w", [P, 2, GROUP], f32))
        ps_h = ctx.enter_context(nc.psum_tensor("ps_h", [P, 2, GROUP], f32))
        ps_m = ctx.enter_context(nc.psum_tensor("ps_m", [P, 2, GROUP], f32))
        M = FEAT + 1

        const_in, bias_in, bias_dve, bias_ready = sem("const_in"), sem("bias_in"), sem("bias_dve"), sem("bias_ready")
        col_in, row_in, idx_dve = sem("col_in"), sem("row_in"), sem("idx_dve")
        row_out, base_out, base_in, prep_done = sem("row_out"), sem("base_out"), sem("base_in"), sem("prep_done")
        zero_set, zeroed = sem("zero_set"), sem("zeroed")
        x_loaded = sems("x_loaded", 2)
        h_mm, h_hi, h_r1, h_mid, h_lo = (sem(n) for n in ("h_mm", "h_hi", "h_r1", "h_mid", "h_lo"))
        h_stored = sems("h_stored", 2)
        rbf_loaded, src_loaded = sems("rbf_loaded", 2), sems("src_loaded", 2)
        dst_loaded, win_loaded = sems("dst_loaded", 2), sems("win_loaded", 2)
        gathered = sems("gathered", 2)
        (z_done, ez_done, y_done, ssp_done, pick_done, same_done, hg_done, hcut_done, w_done, msg_done,
         merge_done, copied, gap_done, idx_done) = (
            sem(n) for n in ("z_done", "ez_done", "y_done", "ssp_done", "pick_done", "same_done", "hg_done",
                             "hcut_done", "w_done", "msg_done", "merge_done", "copied", "gap_done", "idx_done"))
        gath_listed = sem("gath_listed")
        az_done, az2_done = sem("az_done"), sem("az2_done")
        added = sems("added", CHAINS)
        acc_loaded, res_loaded, out_stored = sems("acc_loaded", 2), sems("res_loaded", 2), sems("out_stored", 2)
        (half_sum, agg_done, aggt_mm, aggt_done, z2_done, ez2_done, y2_done, ssp2_done, o_done, res_done,
         stat_done, var_done, ln_done, r0_done, newton, norm_done) = (
            sem(n) for n in ("half_sum", "agg_done", "aggt_mm", "aggt_done", "z2_done", "ez2_done", "y2_done",
                             "ssp2_done", "o_done", "res_done", "stat_done", "var_done", "ln_done", "r0_done",
                             "newton", "norm_done"))
        CONST_DMAS, COL_DMAS, PREP_STEPS = 8, 3, 11

        def group(i, c):
            return i * 4 + c

        def section(i, c):
            return i * 2 + c // 2

        def section_loads(i, c):
            return (i + (c // 4 + 1)) * 16

        def exists(i, c):
            return not isinstance(i, int) or 0 <= 4 * i + c < GROUPS

        def needed(value):
            return not isinstance(value, int) or value > 0

        def over_edges(engine, step, lead, lag):
            for c in range(-lead, 4):
                step(0, c)
            with engine.Fori(1, ROUNDS - 1) as i:
                for c in range(4):
                    step(i, c)
            for c in range(4 + lag):
                step(ROUNDS - 1, c)

        def over_batches(engine, step):
            step(0, 0, 0)
            step(1, 1, 0)
            with engine.Fori(1, BATCHES // 2) as i:
                step(i * 2, 0, i)
                step(i * 2 + 1, 1, i)
            step(BATCHES - 1, 0, BATCHES // 2)

        block = ctx.enter_context(nc.Block())

        @block.sync
        def _(sp):
            sp.dma_start(row32[:, 0, :], src_row).then_inc(row_in, 16)
            sp.dma_start(row32[:, 1, :], dst_row).then_inc(row_in, 16)
            sp.dma_start(w_in_sb[:, :], w_in).then_inc(const_in, 16)
            sp.dma_start(lane_sb[:, :], lane).then_inc(const_in, 16)
            sp.dma_start(w_f2_sb[:, :], w_f2).then_inc(const_in, 16)
            sp.dma_start(w_o1_sb[:, :], w_o1).then_inc(const_in, 16)
            sp.dma_start(w_o2_sb[:, :], w_o2).then_inc(const_in, 16)
            sp.dma_start(eye_sb[:, :], eye).then_inc(const_in, 16)
            sp.dma_start(w_f1_sb[0:RBF, :], w_f1).then_inc(const_in, 16)
            sp.dma_start(w_f1_sb[RBF:RBF + 1, :], b_f1).then_inc(const_in, 16)
            for k, b in enumerate((b_f2, b_o1, b_o2)):
                for r in range(4):
                    sp.dma_start(bias_row[:, k, r * FEAT:(r + 1) * FEAT], b).then_inc(bias_in, 16)

            def h_load(b, slot, use):
                if needed(use):
                    sp.wait_ge(h_mm, b - 1)
                    sp.nop(nofuse=True)
                sp.dma_start(x_in[:, slot, :], x_cols[:, ds(b * BATCH, BATCH)]).then_inc(x_loaded[slot], 16)
            def h_store(b, slot, use):
                sp.wait_ge(h_lo, b + 1)
                sp.nop(nofuse=True)
                sp.dma_start(h_parts[ds(b * BATCH, BATCH), :].rearrange("(p k) f -> p (k f)", k=4),
                             h_out[:, slot, :, :, :].rearrange("p k t f -> p (k t f)")).then_inc(h_stored[slot], 16)
            h_load(0, 0, 0)
            h_load(1, 1, 0)
            sp.wait_ge(bias_dve, 4)
            for t in range(PARTS):
                sp.dma_start(bias3[t:t + 1, :, :].rearrange("o b e -> o (b e)"),
                             bias_part[:, t, :]).then_inc(bias_ready, 16)
            sp.wait_ge(idx_dve, 2)
            sp.dma_start(src16.rearrange("(p a) e -> p (a e)", a=2), row16[:, 0, :]).then_inc(row_out, 16)
            sp.dma_start(dst16.rearrange("(p a) e -> p (a e)", a=2), row16[:, 1, :]).then_inc(row_out, 16)
            sp.wait_ge(idx_dve, 6)
            sp.dma_start(base_dram.rearrange("o (p a) -> (o p) a", a=2), base_f[:, :]).then_inc(base_out, 16)
            sp.dma_start(span_dram.rearrange("o (p a) -> (o p) a", a=2), span_f[:, :]).then_inc(base_out, 16)
            sp.wait_ge(base_out, 32)
            sp.dma_start(span_row[:, :], span_dram).then_inc(base_in, 16)
            sp.dma_start(base_lane[:, :], base_dram.to_broadcast([P, SECTIONS])).then_inc(base_in, 16)
            sp.dma_start(cut_sb[:, :], cut_col).then_inc(col_in, 16)
            sp.dma_start(src_raw[:, :], src_col).then_inc(col_in, 16)
            sp.dma_start(dst_idx[:, :], dst_col).then_inc(col_in, 16)
            with sp.Fori(1, BATCHES // 2) as i:
                h_store(i * 2 - 2, 0, i)
                h_load(i * 2, 0, i)
                h_store(i * 2 - 1, 1, i)
                h_load(i * 2 + 1, 1, i)
            h_store(BATCHES - 3, 0, BATCHES // 2)
            h_load(BATCHES - 1, 0, BATCHES // 2)
            h_store(BATCHES - 2, 1, BATCHES // 2)
            h_store(BATCHES - 1, 0, BATCHES // 2)
            sp.wait_ge(h_stored[0], 16 * (BATCHES // 2 + 1))
            sp.wait_ge(h_stored[1], 16 * (BATCHES // 2))
            sp.wait_ge(row_out, 32)
            sp.wait_ge(prep_done, PREP_STEPS)

            def load_section(i, c, windows):
                slot, before = (c // 2) % 2, group(i, c) - 2
                if windows:
                    first = sp.value_load(base_reg[0:1, ds(section(i, c), 1)], min_val=0, max_val=ROWS - P)
                if needed(before):
                    sp.wait_ge(z_done, before)
                    sp.nop(nofuse=True)
                sp.dma_start(rbf_in[:, slot, :], rbf_t[:, ds(section(i, c) * SECTION, SECTION)]).then_inc(
                    rbf_loaded[slot], 16)
                if needed(before):
                    sp.wait_ge(pick_done, before)
                    sp.nop(nofuse=True)
                sp.dma_start(dst_rep[:, slot, :], dst16[ds(section(i, c), 1), :].to_broadcast([P, SECTION])).then_inc(
                    dst_loaded[slot], 16)
                if windows:
                    if needed(before):
                        sp.wait_ge(hg_done, before)
                        sp.nop(nofuse=True)
                    sp.dma_start(h_win[:, slot, :, :].rearrange("p t f -> p (t f)"),
                                 h_parts[ds(first, P), :]).then_inc(win_loaded[slot], 16)
                if needed(before):
                    sp.wait_ge(same_done, before)
                    sp.nop(nofuse=True)
                sp.dma_start(src_rep[:, slot, :], src16[ds(section(i, c), 1), :].to_broadcast([P, SECTION])).then_inc(
                    src_loaded[slot], 16)

            def load_all(windows):
                load_section(0, 0, windows)
                load_section(0, 2, windows)
                with sp.Fori(1, ROUNDS) as i:
                    load_section(i, 0, windows)
                    load_section(i, 2, windows)

            wide = sp.value_load(wide_flag[0:1, 0:1], min_val=0, max_val=1)
            with sp.If(wide < 1):
                load_all(True)
            with sp.Else():
                load_all(False)

            for q in range(CHAINS):
                sp.wait_ge(added[q], 16 * GROUPS)

            def out_load(b, slot, use):
                if needed(use):
                    sp.wait_ge(half_sum, b - 1)
                    sp.nop(nofuse=True)
                for q in range(CHAINS):
                    sp.dma_start(acc_in[:, slot, q, :],
                                 accum[q][ds(b * BATCH, BATCH), :].rearrange("(p k) f -> p (k f)", k=4)).then_inc(
                        acc_loaded[slot], 16)
                if needed(use):
                    sp.wait_ge(res_done, b - 1)
                    sp.nop(nofuse=True)
                sp.dma_start(x_in[:, slot, :],
                             x_rows[ds(b * BATCH, BATCH), :].rearrange("(p k) f -> p (k f)", k=4)).then_inc(
                    res_loaded[slot], 16)
            over_batches(sp, out_load)

        @block.gpsimd
        def _(pool):
            nc.gpsimd.memset(zero_rows[:, :, :], 0.0).then_inc(zero_set, 1)
            pool.wait_ge(zero_set, 1)
            rows_each = ROWS // P
            for q in range(CHAINS):
                for r in range(0, rows_each, 20):
                    nc.gpsimd.dma_start(accum[q].rearrange("(p r) f -> p r f", r=rows_each)[:, r:r + 20, :],
                                        zero_rows[:, :, :]).then_inc(zeroed, 16)
            pool.wait_ge(zeroed, 16 * CHAINS * (rows_each // 20))
            pool.wait_ge(prep_done, PREP_STEPS)
            pool.wait_ge(col_in, 16 * COL_DMAS)
            pool.wait_ge(h_stored[0], 16 * (BATCHES // 2 + 1))
            pool.wait_ge(h_stored[1], 16 * (BATCHES // 2))

            def scatter(i, c):
                if not exists(i, c):
                    return
                pool.wait_ge(copied, group(i, c) + 1)
                pool.wait_ge(idx_done, group(i, c) + 1)
                for q in range(TILES_PER_GROUP):
                    if needed(group(i, c)):
                        pool.wait_ge(added[q], group(i, c) * 16)
                        pool.nop(nofuse=True)
                    nc.gpsimd.indirect_dma_start(
                        out=accum[q],
                        out_offset=bass.IndirectOffsetOnAxis(ap=row_idx[:, c % 4, q:q + 1].bitcast(u32), axis=0),
                        in_=merged[:, (c % 2) * 4 + q, :], in_offset=None,
                        compute_op=ALU.add).then_inc(added[q], 16)

            def gather(i, c):
                if not exists(i, c):
                    return
                if needed(group(i, c) - 1):
                    pool.wait_ge(hg_done, group(i, c) - 1)
                nc.gpsimd.tensor_copy(gath_idx[:, c % 2, :], dst_idx[:, ds(group(i, c) * 4, 4)]).then_inc(gath_listed, 1)
                pool.wait_ge(gath_listed, group(i, c) + 1)
                pool.nop(nofuse=True)
                for q in range(TILES_PER_GROUP):
                    nc.gpsimd.indirect_dma_start(
                        out=gath[:, c % 2, q, :], out_offset=None, in_=h_parts,
                        in_offset=bass.IndirectOffsetOnAxis(
                            ap=gath_idx[:, c % 2, q:q + 1].bitcast(u32), axis=0),
                    ).then_inc(gathered[c % 2], 16)

            def general(i, c):
                gather(i, c + 2)
                scatter(i, c)

            wide = pool.value_load(wide_flag[0:1, 0:1], min_val=0, max_val=1)
            with pool.If(wide < 1):
                over_edges(pool, scatter, 0, 0)
            with pool.Else():
                over_edges(pool, general, 2, 0)

            def half_sums(b, slot, use):
                pool.wait_ge(acc_loaded[slot], (use + 1) * 16 * CHAINS)
                if needed(use):
                    pool.wait_ge(agg_done, b - 1)
                nc.gpsimd.tensor_tensor(acc_half[:, slot, 0, :], acc_in[:, slot, 0, :], acc_in[:, slot, 1, :], ALU.add)
                nc.gpsimd.tensor_tensor(acc_half[:, slot, 1, :], acc_in[:, slot, 2, :], acc_in[:, slot, 3, :],
                                        ALU.add).then_inc(half_sum, 1)
            over_batches(pool, half_sums)

        @block.tensor
        def _(pe):
            pe.wait_ge(const_in, 16 * CONST_DMAS)

            def h_product(b, slot, use):
                pe.wait_ge(x_loaded[slot], (use + 1) * 16)
                if needed(use):
                    pe.wait_ge(h_r1, b - 1)
                for k in range(4):
                    last = nc.tensor.matmul(ps_z[:, slot, k * FEAT:(k + 1) * FEAT],
                                            x_in[:, slot, k * P:(k + 1) * P], w_in_sb[:, :], start=True, stop=True)
                last.then_inc(h_mm, 1)
            over_batches(pe, h_product)
            pe.wait_ge(h_r1, BATCHES)
            pe.wait_ge(bias_ready, 16 * 3)
            pe.wait_ge(prep_done, PREP_STEPS)

            def filter_in(i, c):
                if not exists(i, c):
                    return
                half = c % 2
                if half == 0:
                    pe.wait_ge(rbf_loaded[(c // 2) % 2], section_loads(i, c))
                if needed(group(i, c) - 1):
                    pe.wait_ge(ssp_done, group(i, c) - 1)
                nc.tensor.matmul(ps_z[:, c % 2, :], w_f1_sb[:, :],
                                 rbf_in[:, (c // 2) % 2, half * GROUP:(half + 1) * GROUP],
                                 start=True, stop=True).then_inc(z_done, 1)

            def pick_rows(i, c, windows):
                if not exists(i, c):
                    return
                if windows:
                    if c % 2 == 0:
                        pe.wait_ge(win_loaded[(c // 2) % 2], section_loads(i, c))
                    pe.wait_ge(pick_done, group(i, c) + 1)
                else:
                    pe.wait_ge(gathered[c % 2], (i * 2 + (c // 2 + 1)) * 64)
                if needed(group(i, c) - 1):
                    pe.wait_ge(hcut_done, group(i, c) - 1)
                for q in range(TILES_PER_GROUP):
                    for t in range(PARTS):
                        if windows:
                            lhs, rhs = pick[:, c % 2, q * P:(q + 1) * P], h_win[:, (c // 2) % 2, t, :]
                        else:
                            lhs, rhs = eye16[:, :], gath[:, c % 2, q, t * FEAT:(t + 1) * FEAT]
                        last = nc.tensor.matmul(ps_h[:, c % 2, q * FEAT:(q + 1) * FEAT], lhs, rhs,
                                                start=(t == 0), stop=(t == PARTS - 1))
                last.then_inc(hg_done, 1)

            def filter_out(i, c):
                if not exists(i, c):
                    return
                pe.wait_ge(ssp_done, group(i, c) + 1)
                if needed(group(i, c) - 1):
                    pe.wait_ge(msg_done, group(i, c) - 1)
                nc.tensor.matmul(ps_w[:, c % 2, :], ones3[:, 0:P], bias3[:, 0, :], start=True, stop=False)
                for q in range(TILES_PER_GROUP):
                    last = nc.tensor.matmul(ps_w[:, c % 2, q * FEAT:(q + 1) * FEAT],
                                            act1[:, c % 2, q * P:(q + 1) * P], w_f2_sb[:, :],
                                            start=False, stop=(q == TILES_PER_GROUP - 1))
                last.then_inc(w_done, 1)

            def merge(i, c):
                if not exists(i, c):
                    return
                pe.wait_ge(same_done, group(i, c) + 1)
                pe.wait_ge(msg_done, group(i, c) + 1)
                if needed(group(i, c)):
                    pe.wait_ge(copied, group(i, c))
                for q in range(TILES_PER_GROUP):
                    last = nc.tensor.matmul(ps_m[:, q // 2, (q % 2) * M:(q % 2 + 1) * M],
                                            same[:, c % 2, q * P:(q + 1) * P], msg[:, c % 2, q, :],
                                            start=True, stop=True)
                last.then_inc(merge_done, 1)

            def edge_step(windows):
                def step(i, c):
                    filter_in(i, c + 1)
                    pick_rows(i, c + 1, windows)
                    filter_out(i, c)
                    merge(i, c - 1)
                return step

            wide = pe.value_load(wide_flag[0:1, 0:1], min_val=0, max_val=1)
            with pe.If(wide < 1):
                over_edges(pe, edge_step(True), 1, 1)
            with pe.Else():
                over_edges(pe, edge_step(False), 1, 1)

            pe.wait_ge(msg_done, GROUPS)
            pe.wait_ge(hcut_done, GROUPS)

            def out_product(b, slot, use):
                pe.wait_ge(agg_done, b + 1)
                if needed(use):
                    pe.wait_ge(aggt_done, b - 1)
                for k in range(4):
                    last = nc.tensor.transpose(ps_z[:, slot, k * P:(k + 1) * P], agg[:, slot, k, :], eye_sb[:, :])
                last.then_inc(aggt_mm, 1)
                pe.wait_ge(aggt_done, b + 1)
                if needed(use):
                    pe.wait_ge(ssp2_done, b - 1)
                nc.tensor.matmul(ps_w[:, slot, :], bias3[:, 1, 0:FEAT], ones3[:, :], start=True, stop=False)
                nc.tensor.matmul(ps_w[:, slot, :], w_o1_sb[:, :], agg_t[:, slot, :],
                                 start=False, stop=True).then_inc(z2_done, 1)
                pe.wait_ge(ssp2_done, b + 1)
                if needed(use):
                    pe.wait_ge(res_done, b - 1)
                nc.tensor.matmul(ps_h[:, slot, :], ones3[:, 0:P], bias3[:, 2, :], start=True, stop=False)
                for k in range(4):
                    last = nc.tensor.matmul(ps_h[:, slot, k * FEAT:(k + 1) * FEAT],
                                            act1[:, slot, k * P:(k + 1) * P], w_o2_sb[:, :],
                                            start=False, stop=(k == 3))
                last.then_inc(o_done, 1)
            over_batches(pe, out_product)

        @block.scalar
        def _(act):
            def h_parts_1_2(b, slot, use):
                act.wait_ge(h_mm, b + 1)
                if needed(use):
                    act.wait_ge(h_stored[slot], use * 16)
                nc.scalar.copy(h_out[:, slot, :, 0, :],
                               ps_z[:, slot, :].rearrange("p (k f) -> p k f", k=4)).then_inc(h_hi, 1)
                act.wait_ge(h_r1, b + 1)
                nc.scalar.copy(h_out[:, slot, :, 1, :], h_rest[:, slot, :, :]).then_inc(h_mid, 1)
            over_batches(act, h_parts_1_2)
            act.wait_ge(col_in, 16 * COL_DMAS)
            act.wait_ge(prep_done, PREP_STEPS)

            def exp_step(i, c):
                if not exists(i, c):
                    return
                act.wait_ge(z_done, group(i, c) + 1)
                if needed(group(i, c) - 1):
                    act.wait_ge(y_done, group(i, c) - 1)
                nc.scalar.activation(az[:, c % 2, :], ps_z[:, c % 2, :], ACT.Abs).then_inc(az_done, 1)
                act.wait_ge(az_done, group(i, c) + 1)
                nc.scalar.activation(ez[:, c % 2, :], az[:, c % 2, :], ACT.Exp, scale=-1.0).then_inc(ez_done, 1)

            def ln_step(i, c):
                if not exists(i, c):
                    return
                act.wait_ge(ez_done, group(i, c) + 1)
                if needed(group(i, c) - 1):
                    act.wait_ge(ssp_done, group(i, c) - 1)
                nc.scalar.activation(yz[:, c % 2, :], ez[:, c % 2, :], ACT.Ln, bias=half_sb[:, 0:1],
                                     scale=0.5).then_inc(y_done, 1)

            def cut_step(i, c):
                if not exists(i, c):
                    return
                act.wait_ge(hg_done, group(i, c) + 1)
                if needed(group(i, c) - 1):
                    act.wait_ge(msg_done, group(i, c) - 1)
                for q in range(TILES_PER_GROUP):
                    last = nc.scalar.activation(h_cut[:, c % 2, q, :], ps_h[:, c % 2, q * FEAT:(q + 1) * FEAT],
                                                ACT.Copy, scale=cut_sb[:, ds(group(i, c) * 4 + q, 1)])
                last.then_inc(hcut_done, 1)

            def copy_merged(i, c):
                if not exists(i, c):
                    return
                act.wait_ge(gap_done, group(i, c) + 1)
                for q in range(TILES_PER_GROUP):
                    if needed(group(i, c) - 1):
                        act.wait_ge(added[q], (group(i, c) - 1) * 16)
                nc.scalar.copy(
                    merged[:, (c % 2) * 4:(c % 2) * 4 + 4, :].rearrange("p (a b) f -> p a b f", a=2),
                    ps_m[:, :, 0:2 * M].rearrange("p a (b m) -> p a b m", m=M)[:, :, :, 0:FEAT]).then_inc(copied, 1)

            def edge_step(i, c):
                exp_step(i, c + 1)
                cut_step(i, c + 1)
                ln_step(i, c + 1)
                copy_merged(i, c - 1)
            over_edges(act, edge_step, 1, 1)

            def out_act(b, slot, use):
                act.wait_ge(aggt_mm, b + 1)
                if needed(use):
                    act.wait_ge(z2_done, b - 1)
                nc.scalar.copy(agg_t[:, slot, :], ps_z[:, slot, :]).then_inc(aggt_done, 1)
                act.wait_ge(z2_done, b + 1)
                if needed(use):
                    act.wait_ge(y2_done, b - 1)
                nc.scalar.activation(az[:, slot, :], ps_w[:, slot, :], ACT.Abs).then_inc(az2_done, 1)
                act.wait_ge(az2_done, b + 1)
                nc.scalar.activation(ez[:, slot, :], az[:, slot, :], ACT.Exp, scale=-1.0).then_inc(ez2_done, 1)
                act.wait_ge(ez2_done, b + 1)
                if needed(use):
                    act.wait_ge(ssp2_done, b - 1)
                nc.scalar.activation(yz[:, slot, :], ez[:, slot, :], ACT.Ln, bias=half_sb[:, 0:1],
                                     scale=0.5).then_inc(y2_done, 1)
                act.wait_ge(stat_done, b + 1)
                if needed(use):
                    act.wait_ge(norm_done, b - 1)
                nc.scalar.activation(rstd[:, slot, 0, :], mean_var[:, slot, :, 1], ACT.Ln,
                                     bias=eps_sb[:, 0:1]).then_inc(ln_done, 1)
                act.wait_ge(ln_done, b + 1)
                nc.scalar.activation(rstd[:, slot, 1, :], rstd[:, slot, 0, :], ACT.Exp, scale=-0.5).then_inc(r0_done, 1)
            def out_store(b, slot, use):
                act.wait_ge(norm_done, b + 1)
                act.dma_start(out[ds(b * BATCH, BATCH), :].rearrange("(p k) f -> p (k f)", k=4),
                              y_out[:, slot, :, :].rearrange("p k f -> p (k f)")).then_inc(out_stored[slot], 16)
            out_act(0, 0, 0)
            out_act(1, 1, 0)
            out_store(0, 0, 0)
            with act.Fori(1, BATCHES // 2) as i:
                out_act(i * 2, 0, i)
                out_store(i * 2 - 1, 1, i)
                out_act(i * 2 + 1, 1, i)
                out_store(i * 2, 0, i)
            out_act(BATCHES - 1, 0, BATCHES // 2)
            out_store(BATCHES - 2, 1, BATCHES // 2)
            left = ATOMS - (BATCHES - 1) * BATCH
            act.wait_ge(norm_done, BATCHES)
            act.dma_start(out[ATOMS - left:ATOMS, :].rearrange("(p k) f -> p (k f)", k=4),
                          y_out[0:left // 4, 0, :, :].rearrange("p k f -> p (k f)")).then_inc(out_stored[0], 16)
            act.wait_ge(out_stored[0], 16 * (BATCHES // 2 + 1))
            act.wait_ge(out_stored[1], 16 * (BATCHES // 2))

        @block.vector
        def _(dve):
            nc.vector.memset(ones3[:, :], 1.0).then_inc(prep_done, 1)
            nc.vector.memset(half_sb[:, :], 0.5).then_inc(prep_done, 1)
            nc.vector.memset(eps_sb[:, :], EPS).then_inc(prep_done, 1)
            dve.wait_ge(row_in, 32)
            nc.vector.tensor_copy(row16[:, 0, :], row32[:, 0, :]).then_inc(idx_dve, 1)
            nc.vector.tensor_copy(row16[:, 1, :], row32[:, 1, :]).then_inc(idx_dve, 1)
            by_section = row32[:, 1, :].rearrange("p (a e) -> p a e", a=2)
            nc.vector.tensor_reduce(top_f[:, :], by_section, AX.X, ALU.max).then_inc(idx_dve, 1)
            nc.vector.tensor_reduce(base_f[:, :], by_section, AX.X, ALU.min).then_inc(idx_dve, 1)
            dve.wait_ge(idx_dve, 4)
            nc.vector.tensor_scalar(base_f[:, :], base_f[:, :], float(ROWS - P), None, ALU.min).then_inc(idx_dve, 1)
            dve.wait_ge(idx_dve, 5)
            nc.vector.tensor_tensor(span_f[:, :], top_f[:, :], base_f[:, :], ALU.subtract).then_inc(idx_dve, 1)
            dve.wait_ge(bias_in, 16 * 12)
            whole = bias_row[:, :, :].rearrange("o b e -> o (b e)")
            rest = bias_rest[:, :, :].rearrange("o b e -> o (b e)")
            nc.vector.tensor_copy(bias_part[:, 0, :], whole).then_inc(bias_dve, 1)
            dve.wait_ge(bias_dve, 1)
            nc.vector.tensor_tensor(rest, whole, bias_part[:, 0, :], ALU.subtract).then_inc(bias_dve, 1)
            dve.wait_ge(bias_dve, 2)
            nc.vector.tensor_copy(bias_part[:, 1, :], rest).then_inc(bias_dve, 1)
            dve.wait_ge(bias_dve, 3)
            nc.vector.tensor_tensor(bias_part[:, 2, :], rest, bias_part[:, 1, :], ALU.subtract).then_inc(bias_dve, 1)
            dve.wait_ge(bias_dve, 4)

            def h_parts_3(b, slot, use):
                dve.wait_ge(h_hi, b + 1)
                nc.vector.tensor_tensor(h_rest[:, slot, :, :], ps_z[:, slot, :].rearrange("p (k f) -> p k f", k=4),
                                        h_out[:, slot, :, 0, :], ALU.subtract).then_inc(h_r1, 1)
                dve.wait_ge(h_mid, b + 1)
                nc.vector.tensor_tensor(h_out[:, slot, :, 2, :], h_rest[:, slot, :, :], h_out[:, slot, :, 1, :],
                                        ALU.subtract).then_inc(h_lo, 1)
            over_batches(dve, h_parts_3)

            dve.wait_ge(const_in, 16 * CONST_DMAS)
            dve.wait_ge(col_in, 16 * COL_DMAS)
            nc.vector.tensor_copy(eye16[:, :], eye_sb[:, :]).then_inc(prep_done, 1)
            nc.vector.tensor_copy(msg[:, :, :, FEAT].rearrange("p a b -> p (a b)"),
                                  lane_sb[:, 2:3].to_broadcast([P, 8])).then_inc(prep_done, 1)
            nc.vector.tensor_copy(src_f[:, :], src_raw[:, :]).then_inc(prep_done, 1)
            nc.vector.tensor_scalar(spare_gap[:, :], src_raw[:, :], -1.0, lane_sb[:, 3:4],
                                    ALU.mult, ALU.add).then_inc(prep_done, 1)
            dve.wait_ge(base_in, 32)
            nc.vector.tensor_copy(base_reg[:, :], base_lane[0:1, :]).then_inc(prep_done, 1)
            nc.vector.tensor_reduce(span_max[:, :], span_row[:, :], AX.X, ALU.max).then_inc(prep_done, 1)
            dve.wait_ge(prep_done, 9)
            nc.vector.tensor_scalar(base_lane[:, :], base_lane[:, :], lane_sb[:, 0:1], None,
                                    ALU.add).then_inc(prep_done, 1)
            nc.vector.tensor_scalar(wide_flag[:, :], span_max[:, :], float(P), None, ALU.is_ge).then_inc(prep_done, 1)
            dve.wait_ge(prep_done, PREP_STEPS)

            def pick_step(i, c):
                if not exists(i, c):
                    return
                half = c % 2
                if half == 0:
                    dve.wait_ge(dst_loaded[(c // 2) % 2], section_loads(i, c))
                if needed(group(i, c) - 1):
                    dve.wait_ge(hg_done, group(i, c) - 1)
                nc.vector.tensor_scalar(pick[:, c % 2, :], dst_rep[:, (c // 2) % 2, half * GROUP:(half + 1) * GROUP],
                                        base_lane[:, ds(section(i, c), 1)], None, ALU.is_equal).then_inc(pick_done, 1)

            def same_step(i, c):
                if not exists(i, c):
                    return
                half = c % 2
                if half == 0:
                    dve.wait_ge(src_loaded[(c // 2) % 2], section_loads(i, c))
                if needed(group(i, c) - 1):
                    dve.wait_ge(merge_done, group(i, c) - 1)
                nc.vector.tensor_tensor(
                    same[:, c % 2, :].rearrange("p (q e) -> p q e", q=4),
                    src_rep[:, (c // 2) % 2, half * GROUP:(half + 1) * GROUP].rearrange("p (q e) -> p q e", q=4),
                    src_f[:, ds(group(i, c) * 4, 4)].unsqueeze(2).to_broadcast([P, 4, P]),
                    ALU.is_equal).then_inc(same_done, 1)

            def ssp_step(i, c):
                if not exists(i, c):
                    return
                dve.wait_ge(y_done, group(i, c) + 1)
                if needed(group(i, c) - 1):
                    dve.wait_ge(w_done, group(i, c) - 1)
                nc.vector.scalar_tensor_tensor(out=act1[:, c % 2, :], in0=ps_z[:, c % 2, :], scalar=0.0,
                                               in1=yz[:, c % 2, :], op0=ALU.max, op1=ALU.add).then_inc(ssp_done, 1)

            def msg_step(i, c):
                if not exists(i, c):
                    return
                dve.wait_ge(w_done, group(i, c) + 1)
                dve.wait_ge(hcut_done, group(i, c) + 1)
                if needed(group(i, c) - 1):
                    dve.wait_ge(merge_done, group(i, c) - 1)
                nc.vector.tensor_tensor(msg[:, c % 2, :, 0:FEAT], ps_w[:, c % 2, :].rearrange("p (q f) -> p q f", q=4),
                                        h_cut[:, c % 2, :, :], ALU.mult).then_inc(msg_done, 1)

            def idx_step(i, c):
                if not exists(i, c):
                    return
                dve.wait_ge(merge_done, group(i, c) + 1)
                nc.vector.scalar_tensor_tensor(
                    out=gap[:, c % 4, :].rearrange("p (a b) -> p a b", a=2),
                    in0=ps_m[:, :, 0:2 * M].rearrange("p a (b m) -> p a b m", m=M)[:, :, :, FEAT],
                    scalar=lane_sb[:, 1:2],
                    in1=spare_gap[:, ds(group(i, c) * 4, 4)].rearrange("p (a b) -> p a b", a=2),
                    op0=ALU.is_ge, op1=ALU.mult).then_inc(gap_done, 1)
                dve.wait_ge(gap_done, group(i, c) + 1)
                for q in range(TILES_PER_GROUP):
                    if needed(group(i, c) - 2):
                        dve.wait_ge(added[q], (group(i, c) - 2) * 16)
                nc.vector.tensor_tensor(row_idx[:, c % 4, :], gap[:, c % 4, :], src_f[:, ds(group(i, c) * 4, 4)],
                                        ALU.add).then_inc(idx_done, 1)

            def edge_step(i, c):
                pick_step(i, c + 2)
                same_step(i, c)
                ssp_step(i, c + 1)
                msg_step(i, c)
                idx_step(i, c - 1)
            over_edges(dve, edge_step, 2, 1)

            def out_step(b, slot, use):
                dve.wait_ge(half_sum, b + 1)
                if needed(use):
                    dve.wait_ge(aggt_mm, b - 1)
                nc.vector.tensor_tensor(agg[:, slot, :, :].rearrange("p k f -> p (k f)"), acc_half[:, slot, 0, :],
                                        acc_half[:, slot, 1, :], ALU.add).then_inc(agg_done, 1)
                dve.wait_ge(y2_done, b + 1)
                if needed(use):
                    dve.wait_ge(o_done, b - 1)
                nc.vector.scalar_tensor_tensor(out=act1[:, slot, :], in0=ps_w[:, slot, :], scalar=0.0,
                                               in1=yz[:, slot, :], op0=ALU.max, op1=ALU.add).then_inc(ssp2_done, 1)
                dve.wait_ge(o_done, b + 1)
                dve.wait_ge(res_loaded[slot], (use + 1) * 16)
                nc.vector.tensor_tensor(res[:, slot, :, :].rearrange("p k f -> p (k f)"), ps_h[:, slot, :],
                                        x_in[:, slot, :], ALU.add).then_inc(res_done, 1)
                dve.wait_ge(res_done, b + 1)
                for k in range(4):
                    last = nc.vector.bn_stats(stats[:, slot, k, :], res[:, slot, k, :])
                last.then_inc(var_done, 1)
                dve.wait_ge(var_done, b + 1)
                dve.nop(nofuse=True)
                for k in range(4):
                    last = nc.vector.bn_aggr(mean_var[:, slot, k, :], stats[:, slot, k, :])
                last.then_inc(stat_done, 1)
                r = [rstd[:, slot, k, :] for k in range(5)]
                dve.wait_ge(r0_done, b + 1)
                nc.vector.tensor_tensor(r[2], r[1], r[1], ALU.mult).then_inc(newton, 1)
                dve.wait_ge(newton, b * 4 + 1)
                nc.vector.scalar_tensor_tensor(out=r[3], in0=mean_var[:, slot, :, 1], scalar=EPS, in1=r[2],
                                               op0=ALU.add, op1=ALU.mult).then_inc(newton, 1)
                dve.wait_ge(newton, b * 4 + 2)
                nc.vector.tensor_scalar(r[4], r[3], -0.5, 1.5, ALU.mult, ALU.add).then_inc(newton, 1)
                dve.wait_ge(newton, b * 4 + 3)
                nc.vector.tensor_tensor(r[2], r[1], r[4], ALU.mult).then_inc(newton, 1)
                dve.wait_ge(newton, b * 4 + 4)
                if needed(use):
                    dve.wait_ge(out_stored[slot], use * 16)
                for k in range(4):
                    last = nc.vector.tensor_scalar(y_out[:, slot, k, :], res[:, slot, k, :], mean_var[:, slot, k, 0:1],
                                                   rstd[:, slot, 2, k:k + 1], ALU.subtract, ALU.mult)
                last.then_inc(norm_done, 1)
            over_batches(dve, out_step)


def kernel(x, src, dst, edge_attr3_1x20, edge_weight1, L0_gnn_W_in, L0_gnn_W_f1, L0_gnn_b_f1, L0_gnn_W_f2,
           L0_gnn_b_f2, L0_gnn_W_o1, L0_gnn_b_o1, L0_gnn_W_o2, L0_gnn_b_o2):
    import concourse.bacc as bacc
    from concourse.bass_utils import run_bass_kernel_spmd

    x, src, dst = np.asarray(x), np.asarray(src), np.asarray(dst)
    more_edges, more_rows = EDGE_ROWS - EDGES, ROWS - ATOMS
    x_rows = np.concatenate([x, np.zeros((more_rows, FEAT), x.dtype)])
    src_all = np.concatenate([src, np.full(more_edges, SPARE, src.dtype)])
    dst_all = np.concatenate([dst, np.full(more_edges, ATOMS - 1, dst.dtype)])
    cut = np.asarray(edge_weight1).reshape(EDGES)
    cut_all = np.concatenate([cut, np.zeros(more_edges, cut.dtype)])
    rbf = np.asarray(edge_attr3_1x20).reshape(EDGES, RBF)
    rbf_t = np.concatenate([np.concatenate([rbf.T, np.zeros((RBF, more_edges), rbf.dtype)], 1),
                            np.ones((1, EDGE_ROWS), rbf.dtype)])
    p = np.arange(P)
    lane = np.stack([p, 2.5 * 2.0 ** (60 - p), 2.0 ** (60 - p), SPARE + p], 1).astype(np.float32)

    def columns(v):
        return np.ascontiguousarray(v.reshape(TILES, P).T)

    arrays = {
        "x_rows": x_rows,
        "x_cols": np.ascontiguousarray(x_rows.reshape(BATCHES, P, 4, FEAT).transpose(3, 0, 2, 1).reshape(FEAT, ROWS)),
        "src_row": src_all.reshape(SECTIONS // 2, 2 * SECTION), "dst_row": dst_all.reshape(SECTIONS // 2, 2 * SECTION),
        "src_col": columns(src_all), "dst_col": columns(dst_all), "cut_col": columns(cut_all),
        "rbf_t": rbf_t,
        "w_in": np.asarray(L0_gnn_W_in), "w_f1": np.asarray(L0_gnn_W_f1),
        "b_f1": np.asarray(L0_gnn_b_f1).reshape(1, FEAT), "w_f2": np.asarray(L0_gnn_W_f2),
        "b_f2": np.asarray(L0_gnn_b_f2).reshape(1, FEAT), "w_o1": np.asarray(L0_gnn_W_o1),
        "b_o1": np.asarray(L0_gnn_b_o1).reshape(1, FEAT), "w_o2": np.asarray(L0_gnn_W_o2),
        "b_o2": np.asarray(L0_gnn_b_o2).reshape(1, FEAT),
        "lane": lane, "eye": np.eye(P, dtype=np.float32),
    }
    nc = bacc.Bacc("TRN2", target_bir_lowering=False, num_devices=1)
    args = [nc.dram_tensor(name, a.shape, mybir.dt.from_np(a.dtype), kind="ExternalInput").ap()
            for name, a in arrays.items()]
    out = nc.dram_tensor("out", (ATOMS, FEAT), mybir.dt.float32, kind="ExternalOutput").ap()
    gnn_program(nc, *args, out)
    result = run_bass_kernel_spmd(nc, [arrays], core_ids=[0])
    return result.results[0]["out"]
```

```python
import numpy as np
import concourse.bass as bass
from concourse import mybir
from contextlib import ExitStack

P = 128
ATOMS, FEAT, EDGES, RBF = 12500, 128, 212500, 20
TILES_PER_GROUP = 4
GROUP = TILES_PER_GROUP * P
SECTION = 2 * GROUP
SECTIONS = -(-EDGES // SECTION)
GROUPS = 2 * SECTIONS
TILES = GROUPS * TILES_PER_GROUP
EDGE_ROWS = SECTIONS * SECTION
BATCH = 4 * P
BATCHES = -(-ATOMS // BATCH)
ROWS = BATCHES * BATCH
SPARE = ROWS - 2 * P
CHAINS = 6
UNROLL = 6
SECTION_SLOTS = 3
ZERO_ROWS = 20
PARTS = 3
MERGED_SLOTS = 3
EPS = 1e-5
assert SPARE >= ATOMS and SECTIONS % 2 == 0
assert UNROLL * TILES_PER_GROUP % CHAINS == 0 and UNROLL % (2 * SECTION_SLOTS) == 0 and UNROLL % MERGED_SLOTS == 0


def gnn_program(nc, x_rows, x_cols, src_row, dst_row, src_col, dst_col, cut_col, rbf_t,
                w_in, w_f1, b_f1, w_f2, b_f2, w_o1, b_o1, w_o2, b_o2, lane, eye, out):
    f32, bf16, i16, i32, u32 = (mybir.dt.float32, mybir.dt.bfloat16, mybir.dt.int16,
                                mybir.dt.int32, mybir.dt.uint32)
    ALU, ACT, AX = mybir.AluOpType, mybir.ActivationFunctionType, mybir.AxisListType
    ds = bass.ds
    ctx = ExitStack()
    with ctx:
        def sb(name, shape, dt):
            return ctx.enter_context(nc.sbuf_tensor(name, shape, dt))

        def sem(name):
            return ctx.enter_context(nc.semaphore(name))

        def sems(name, n):
            return [sem(f"{name}{k}") for k in range(n)]

        h_parts = nc.dram_tensor("h_parts", [ROWS, PARTS * FEAT], bf16).ap()
        src16 = nc.dram_tensor("src16", [SECTIONS, SECTION], i16).ap()
        dst16 = nc.dram_tensor("dst16", [SECTIONS, SECTION], i16).ap()
        base_dram = nc.dram_tensor("base_dram", [1, SECTIONS], f32).ap()
        span_dram = nc.dram_tensor("span_dram", [1, SECTIONS], f32).ap()
        accum = [nc.dram_tensor(f"accum{q}", [ROWS, FEAT], f32).ap() for q in range(CHAINS)]

        w_in_sb = sb("w_in_sb", [P, FEAT], f32)
        w_f1_sb = sb("w_f1_sb", [P, FEAT], f32)
        w_f2_sb = sb("w_f2_sb", [P, FEAT], f32)
        w_o1_sb = sb("w_o1_sb", [P, FEAT], f32)
        w_o2_sb = sb("w_o2_sb", [P, FEAT], f32)
        eye_sb = sb("eye_sb", [P, P], f32)
        eye16 = sb("eye16", [P, P], bf16)
        lane_sb = sb("lane_sb", [P, 4], f32)
        ones16 = sb("ones16", [P, GROUP], bf16)
        shared_a = sb("shared_a", [P, 3 * GROUP * 7 // 2], f32)
        bias_row = shared_a[0:1, 0:3 * GROUP]
        bias_rest = shared_a[0:1, 3 * GROUP:6 * GROUP]
        bias_part = shared_a[0:1, 6 * GROUP:].bitcast(bf16).rearrange("o (t e) -> o t e", t=PARTS)
        acc_part = shared_a[:, 0:2 * 3 * 4 * FEAT].rearrange("p (s n e) -> p s n e", s=2, n=3)
        bias3 = sb("bias3", [P, 3, GROUP], bf16)
        zero_rows = sb("zero_rows", [P, ZERO_ROWS, FEAT], f32)
        cut_sb = sb("cut_sb", [P, TILES], f32)
        src_raw = sb("src_raw", [P, TILES], i32)
        src_f = sb("src_f", [P, TILES], f32)
        spare_gap = sb("spare_gap", [P, TILES], f32)
        dst_idx = sb("dst_idx", [P, TILES], i32)
        base_lane = sb("base_lane", [P, SECTIONS], f32)
        base_reg = sb("base_reg", [1, SECTIONS], i32)
        span_row = sb("span_row", [1, SECTIONS], f32)
        span_max = sb("span_max", [1, 1], f32)
        wide_flag = sb("wide_flag", [1, 1], i32)
        HALF = SECTIONS // 2
        shared_b = sb("shared_b", [P, 6 * SECTION], f32)
        row32 = shared_b[0:HALF, 0:4 * SECTION].bitcast(i32).rearrange("p (a e) -> p a e", a=2)
        row16 = shared_b[0:HALF, 4 * SECTION:].bitcast(i16).rearrange("p (a e) -> p a e", a=2)
        acc_in = shared_b[:, 0:2 * CHAINS * 4 * FEAT].rearrange("p (s q e) -> p s q e", s=2, q=CHAINS)
        base_f = sb("base_f", [HALF, 2], f32)
        top_f = sb("top_f", [HALF, 2], f32)
        span_f = sb("span_f", [HALF, 2], f32)

        rbf_in = sb("rbf_in", [P, SECTION_SLOTS, SECTION], f32)
        src_rep = sb("src_rep", [P, SECTION_SLOTS, SECTION], i16)
        dst_rep = sb("dst_rep", [P, SECTION_SLOTS, SECTION], i16)
        h_win = sb("h_win", [P, SECTION_SLOTS, PARTS, FEAT], bf16)
        pick = sb("pick", [P, 2, GROUP], bf16)
        same = sb("same", [P, 2, GROUP], f32)
        az = sb("az", [P, 2, GROUP], f32)
        ez = sb("ez", [P, 2, GROUP], f32)
        yz = sb("yz", [P, 2, GROUP], f32)
        act1 = sb("act1", [P, 2, GROUP], f32)
        h_cut = sb("h_cut", [P, 2, TILES_PER_GROUP, FEAT], f32)
        msg = sb("msg", [P, 2, TILES_PER_GROUP, FEAT + 1], f32)
        merged = sb("merged", [P, MERGED_SLOTS, TILES_PER_GROUP, FEAT], f32)
        gap = sb("gap", [P, MERGED_SLOTS, TILES_PER_GROUP], f32)
        row_idx = sb("row_idx", [P, MERGED_SLOTS, TILES_PER_GROUP], i32)
        gath_idx = sb("gath_idx", [P, 2, TILES_PER_GROUP], i32)
        gath = sb("gath", [P, 2, TILES_PER_GROUP, PARTS * FEAT], bf16)

        x_in = sb("x_in", [P, 2, BATCH], f32)
        h_out = sb("h_out", [P, 2, 4, PARTS, FEAT], bf16)
        h_rest = sb("h_rest", [P, 2, 4, FEAT], f32)
        agg = sb("agg", [P, 2, 4, FEAT], f32)
        agg_t = sb("agg_t", [P, 2, BATCH], f32)
        res = sb("res", [P, 2, 4, FEAT], f32)
        stats = sb("stats", [P, 2, 4, 6], f32)
        mean_var = sb("mean_var", [P, 2, 4, 2], f32)
        rstd = sb("rstd", [P, 2, 5, 4], f32)
        y_out = h_rest
        eps_sb = sb("eps_sb", [P, 1], f32)
        half_sb = sb("half_sb", [P, 1], f32)

        ps_z = ctx.enter_context(nc.psum_tensor("ps_z", [P, 2, GROUP], f32))
        ps_w = ctx.enter_context(nc.psum_tensor("ps_w", [P, 2, GROUP], f32))
        ps_h = ctx.enter_context(nc.psum_tensor("ps_h", [P, 2, GROUP], f32))
        ps_m = ctx.enter_context(nc.psum_tensor("ps_m", [P, 2, GROUP], f32))
        M = FEAT + 1

        const_in, bias_in, bias_dve, bias_ready = sem("const_in"), sem("bias_in"), sem("bias_dve"), sem("bias_ready")
        col_in, row_in, idx_dve = sem("col_in"), sem("row_in"), sem("idx_dve")
        row_out, base_out, base_in, prep_done = sem("row_out"), sem("base_out"), sem("base_in"), sem("prep_done")
        zero_set, zeroed = sem("zero_set"), sems("zeroed", CHAINS)
        w_in_loaded, padded = sem("w_in_loaded"), sem("padded")
        x_loaded = sems("x_loaded", 2)
        h_mm, h_hi, h_r1, h_mid, h_lo = (sem(n) for n in ("h_mm", "h_hi", "h_r1", "h_mid", "h_lo"))
        h_stored = sems("h_stored", 2)
        rbf_loaded, src_loaded = sems("rbf_loaded", SECTION_SLOTS), sems("src_loaded", SECTION_SLOTS)
        dst_loaded, win_loaded = sems("dst_loaded", SECTION_SLOTS), sems("win_loaded", SECTION_SLOTS)
        gathered = sems("gathered", 2)
        (z_done, ez_done, y_done, ssp_done, pick_done, same_done, hg_done, hcut_done, w_done, msg_done,
         merge_done, copied, gap_done, idx_done) = (
            sem(n) for n in ("z_done", "ez_done", "y_done", "ssp_done", "pick_done", "same_done", "hg_done",
                             "hcut_done", "w_done", "msg_done", "merge_done", "copied", "gap_done", "idx_done"))
        gath_listed = sem("gath_listed")
        az_done, az2_done = sem("az_done"), sem("az2_done")
        added = sems("added", CHAINS)
        acc_loaded, res_loaded, out_stored = sems("acc_loaded", 2), sems("res_loaded", 2), sems("out_stored", 2)
        (pair_sums, part_sum, agg_done, aggt_mm, aggt_done, z2_done, ez2_done, y2_done, ssp2_done, o_done, res_done,
         stat_done, var_done, ln_done, r0_done, newton, shift_done, norm_done) = (
            sem(n) for n in ("pair_sums", "part_sum", "agg_done", "aggt_mm", "aggt_done", "z2_done", "ez2_done", "y2_done",
                             "ssp2_done", "o_done", "res_done", "stat_done", "var_done", "ln_done", "r0_done",
                             "newton", "shift_done", "norm_done"))
        CONST_DMAS, COL_DMAS, PREP_STEPS = 7, 3, 11

        def group(i, c):
            return i * UNROLL + c

        def section(i, c):
            return i * (UNROLL // 2) + c // 2

        def section_slot(c):
            return c // 2 % SECTION_SLOTS

        def section_loads(i, c):
            return (i * (UNROLL // 2 // SECTION_SLOTS) + (c // 2 // SECTION_SLOTS + 1)) * 16

        def chain(c, q):
            return (c * TILES_PER_GROUP + q) % CHAINS

        def chain_scatters(i, c, q):
            return i * (UNROLL * TILES_PER_GROUP // CHAINS) + (c * TILES_PER_GROUP + q) // CHAINS

        def exists(i, c):
            return not isinstance(i, int) or 0 <= UNROLL * i + c < GROUPS

        def there(i, c):
            return not isinstance(i, int) or 0 <= 2 * i + c < BATCHES

        def needed(value):
            return not isinstance(value, int) or value > 0

        def pipeline(engine, step, count, unroll, lead, lag):
            first, last = -(-(lag + 3) // unroll), (count - lead) // unroll
            for c in range(-lead, unroll * first):
                step(0, c)
            with engine.Fori(first, last) as i:
                for c in range(unroll):
                    step(i, c)
            for c in range(count - unroll * last + lag):
                step(last, c)

        def over_edges(engine, step, lead, lag):
            pipeline(engine, step, GROUPS, UNROLL, lead, lag)

        def over_batches(engine, step, lead=0, lag=0):
            pipeline(engine, step, BATCHES, 2, lead, lag)

        block = ctx.enter_context(nc.Block())

        @block.sync
        def _(sp):
            def h_load(i, c):
                if not there(i, c):
                    return
                b = i * 2 + c
                if needed(b - 1):
                    sp.wait_ge(h_mm, b - 1)
                    sp.nop(nofuse=True)
                sp.dma_start(x_in[:, c % 2, :], x_cols[:, ds(b * BATCH, BATCH)]).then_inc(x_loaded[c % 2], 16)

            def h_store(i, c):
                if not there(i, c):
                    return
                b = i * 2 + c
                sp.wait_ge(h_lo, b + 1)
                sp.nop(nofuse=True)
                sp.dma_start(h_parts[ds(b * BATCH, BATCH), :].rearrange("(p k) f -> p (k f)", k=4),
                             h_out[:, c % 2, :, :, :].rearrange("p k t f -> p (k t f)")).then_inc(h_stored[c % 2], 16)

            def h_step(i, c):
                h_load(i, c + 2)
                h_store(i, c)

            sp.dma_start(w_in_sb[:, :], w_in).then_inc(w_in_loaded, 16)
            over_batches(sp, h_step, lead=2)
            sp.wait_ge(h_stored[0], 16 * (BATCHES // 2 + 1))
            sp.wait_ge(h_stored[1], 16 * (BATCHES // 2))
            sp.wait_ge(row_out, 32)
            sp.wait_ge(prep_done, PREP_STEPS)

            def load_section(i, c, windows):
                slot, before = section_slot(c), group(i, c) - 2 * SECTION_SLOTS + 2
                if windows:
                    first = sp.value_load(base_reg[0:1, ds(section(i, c), 1)], min_val=0, max_val=ROWS - P)
                if needed(before):
                    sp.wait_ge(z_done, before)
                    sp.nop(nofuse=True)
                sp.dma_start(rbf_in[0:RBF + 1, slot, :], rbf_t[:, ds(section(i, c) * SECTION, SECTION)]).then_inc(
                    rbf_loaded[slot], 16)
                if needed(before):
                    sp.wait_ge(pick_done, before)
                    sp.nop(nofuse=True)
                sp.dma_start(dst_rep[:, slot, :], dst16[ds(section(i, c), 1), :].to_broadcast([P, SECTION])).then_inc(
                    dst_loaded[slot], 16)
                if windows:
                    if needed(before):
                        sp.wait_ge(hg_done, before)
                        sp.nop(nofuse=True)
                    sp.dma_start(h_win[:, slot, :, :].rearrange("p t f -> p (t f)"),
                                 h_parts[ds(first, P), :]).then_inc(win_loaded[slot], 16)
                if needed(before):
                    sp.wait_ge(same_done, before)
                    sp.nop(nofuse=True)
                sp.dma_start(src_rep[:, slot, :], src16[ds(section(i, c), 1), :].to_broadcast([P, SECTION])).then_inc(
                    src_loaded[slot], 16)

            def load_all(windows):
                def step(i, c):
                    if exists(i, c) and c % 2 == 0:
                        load_section(i, c, windows)
                over_edges(sp, step, 0, 0)

            sp.wait_ge(padded, 3)
            wide = sp.value_load(wide_flag[0:1, 0:1], min_val=0, max_val=1)
            with sp.If(wide < 1):
                load_all(True)
            with sp.Else():
                load_all(False)

            for q in range(CHAINS):
                sp.wait_ge(added[q], 16 * len(range(q, TILES, CHAINS)))

            def acc_load(i, c):
                if not there(i, c):
                    return
                b = i * 2 + c
                if needed(b - 1):
                    sp.wait_ge(pair_sums, b - 1)
                    sp.nop(nofuse=True)
                for q in range(CHAINS):
                    sp.dma_start(acc_in[:, c % 2, q, :],
                                 accum[q][ds(b * BATCH, BATCH), :].rearrange("(p k) f -> p (k f)", k=4)).then_inc(
                        acc_loaded[c % 2], 16)

            def res_load(i, c):
                if not there(i, c):
                    return
                b = i * 2 + c
                if needed(b - 1):
                    sp.wait_ge(res_done, b - 1)
                    sp.nop(nofuse=True)
                sp.dma_start(x_in[:, c % 2, :],
                             x_rows[ds(b * BATCH, BATCH), :].rearrange("(p k) f -> p (k f)", k=4)).then_inc(
                    res_loaded[c % 2], 16)

            def out_store(i, c):
                if not there(i, c):
                    return
                b = i * 2 + c
                sp.wait_ge(norm_done, b + 1)
                sp.nop(nofuse=True)
                rows = BATCH
                if isinstance(i, int) and b == BATCHES - 1:
                    rows = ATOMS - b * BATCH
                sp.dma_start(out[ds(b * BATCH, rows), :].rearrange("(p k) f -> p (k f)", k=4),
                             y_out[0:rows // 4, c % 2, :, :].rearrange("p k f -> p (k f)")).then_inc(
                    out_stored[c % 2], 16)

            def out_step(i, c):
                acc_load(i, c + 2)
                res_load(i, c)
                out_store(i, c - 3)
            over_batches(sp, out_step, lead=2, lag=3)
            sp.wait_ge(out_stored[0], 16 * (BATCHES // 2 + 1))
            sp.wait_ge(out_stored[1], 16 * (BATCHES // 2))

        @block.gpsimd
        def _(pool):
            nc.gpsimd.memset(w_f1_sb[:, :], 0.0).then_inc(padded, 1)
            nc.gpsimd.memset(bias3[:, :, :], 0.0).then_inc(padded, 1)
            pool.dma_start(row32[:, 0, :], src_row).then_inc(row_in, 16)
            pool.dma_start(row32[:, 1, :], dst_row).then_inc(row_in, 16)
            pool.dma_start(lane_sb[:, :], lane).then_inc(const_in, 16)
            for k, b in enumerate((b_f2, b_o1, b_o2)):
                pool.dma_start(bias_row[:, k * GROUP:(k + 1) * GROUP].rearrange("o (r f) -> o r f", r=4),
                               b.unsqueeze(1).to_broadcast([1, 4, FEAT])).then_inc(bias_in, 16)
            pool.dma_start(eye_sb[:, :], eye).then_inc(const_in, 16)
            pool.dma_start(src_raw[:, :], src_col).then_inc(col_in, 16)
            pool.dma_start(cut_sb[:, :], cut_col).then_inc(col_in, 16)
            pool.dma_start(dst_idx[:, :], dst_col).then_inc(col_in, 16)
            pool.wait_ge(padded, 2)
            pool.dma_start(w_f1_sb[0:RBF, :], w_f1).then_inc(const_in, 16)
            pool.dma_start(w_f1_sb[RBF:RBF + 1, :], b_f1).then_inc(const_in, 16)
            pool.dma_start(w_f2_sb[:, :], w_f2).then_inc(const_in, 16)
            pool.dma_start(w_o1_sb[:, :], w_o1).then_inc(const_in, 16)
            pool.dma_start(w_o2_sb[:, :], w_o2).then_inc(const_in, 16)
            nc.gpsimd.memset(zero_rows[:, :, :], 0.0).then_inc(zero_set, 1)
            nc.gpsimd.memset(rbf_in[:, :, :], 0.0).then_inc(padded, 1)
            pool.wait_ge(idx_dve, 2)
            pool.dma_start(src16.rearrange("(p a) e -> p (a e)", a=2), row16[:, 0, :]).then_inc(row_out, 16)
            pool.dma_start(dst16.rearrange("(p a) e -> p (a e)", a=2), row16[:, 1, :]).then_inc(row_out, 16)
            pool.wait_ge(idx_dve, 6)
            pool.dma_start(base_dram.rearrange("o (p a) -> (o p) a", a=2), base_f[:, :]).then_inc(base_out, 16)
            pool.dma_start(span_dram.rearrange("o (p a) -> (o p) a", a=2), span_f[:, :]).then_inc(base_out, 16)
            pool.wait_ge(bias_dve, 4)
            for t in range(PARTS):
                pool.dma_start(bias3[t:t + 1, :, :].rearrange("o b e -> o (b e)"),
                               bias_part[:, t, :]).then_inc(bias_ready, 16)
            pool.wait_ge(base_out, 32)
            pool.dma_start(span_row[:, :], span_dram).then_inc(base_in, 16)
            pool.dma_start(base_lane[:, :], base_dram.to_broadcast([P, SECTIONS])).then_inc(base_in, 16)
            pool.wait_ge(zero_set, 1)
            rows_each = ROWS // P
            for q in range(CHAINS):
                for r in range(0, rows_each, ZERO_ROWS):
                    pool.dma_start(accum[q].rearrange("(p r) f -> p r f", r=rows_each)[:, r:r + ZERO_ROWS, :],
                                   zero_rows[:, :, :]).then_inc(zeroed[q], 16)
            pool.wait_ge(prep_done, PREP_STEPS)
            pool.wait_ge(col_in, 16 * COL_DMAS)
            pool.wait_ge(h_stored[0], 16 * (BATCHES // 2 + 1))
            pool.wait_ge(h_stored[1], 16 * (BATCHES // 2))

            def scatter(i, c):
                if not exists(i, c):
                    return
                pool.wait_ge(copied, group(i, c) + 1)
                pool.wait_ge(idx_done, group(i, c) + 1)
                for q in range(TILES_PER_GROUP):
                    k = chain(c, q)
                    if needed(chain_scatters(i, c, q)):
                        pool.wait_ge(added[k], chain_scatters(i, c, q) * 16)
                        pool.nop(nofuse=True)
                    else:
                        pool.wait_ge(zeroed[k], 16 * (ROWS // P // ZERO_ROWS))
                    nc.gpsimd.indirect_dma_start(
                        out=accum[k],
                        out_offset=bass.IndirectOffsetOnAxis(
                            ap=row_idx[:, c % MERGED_SLOTS, q:q + 1].bitcast(u32), axis=0),
                        in_=merged[:, c % MERGED_SLOTS, q, :], in_offset=None,
                        compute_op=ALU.add).then_inc(added[k], 16)

            def gather(i, c):
                if not exists(i, c):
                    return
                if needed(group(i, c) - 1):
                    pool.wait_ge(hg_done, group(i, c) - 1)
                nc.gpsimd.tensor_copy(gath_idx[:, c % 2, :], dst_idx[:, ds(group(i, c) * 4, 4)]).then_inc(gath_listed, 1)
                pool.wait_ge(gath_listed, group(i, c) + 1)
                pool.nop(nofuse=True)
                for q in range(TILES_PER_GROUP):
                    nc.gpsimd.indirect_dma_start(
                        out=gath[:, c % 2, q, :], out_offset=None, in_=h_parts,
                        in_offset=bass.IndirectOffsetOnAxis(
                            ap=gath_idx[:, c % 2, q:q + 1].bitcast(u32), axis=0),
                    ).then_inc(gathered[c % 2], 16)

            def general(i, c):
                gather(i, c + 2)
                scatter(i, c)

            wide = pool.value_load(wide_flag[0:1, 0:1], min_val=0, max_val=1)
            with pool.If(wide < 1):
                over_edges(pool, scatter, 0, 0)
            with pool.Else():
                over_edges(pool, general, 2, 0)

            def add_pairs(i, c):
                if not there(i, c):
                    return
                b, slot = i * 2 + c, c % 2
                pool.wait_ge(acc_loaded[slot], (i + (c // 2 + 1)) * 16 * CHAINS)
                if needed(b - 1):
                    pool.wait_ge(agg_done, b - 1)
                for k in range(3):
                    last = nc.gpsimd.tensor_tensor(acc_part[:, slot, k, :], acc_in[:, slot, 2 * k, :],
                                                   acc_in[:, slot, 2 * k + 1, :], ALU.add)
                last.then_inc(pair_sums, 1)
            over_batches(pool, add_pairs)

        @block.tensor
        def _(pe):
            pe.wait_ge(w_in_loaded, 16)

            def h_product(i, c):
                if not there(i, c):
                    return
                b, slot = i * 2 + c, c % 2
                pe.wait_ge(x_loaded[slot], (i + (c // 2 + 1)) * 16)
                if needed(b - 1):
                    pe.wait_ge(h_r1, b - 1)
                for k in range(4):
                    last = nc.tensor.matmul(ps_z[:, slot, k * FEAT:(k + 1) * FEAT],
                                            x_in[:, slot, k * P:(k + 1) * P], w_in_sb[:, :], start=True, stop=True)
                last.then_inc(h_mm, 1)
            over_batches(pe, h_product)
            pe.wait_ge(h_r1, BATCHES)
            pe.wait_ge(const_in, 16 * CONST_DMAS)
            pe.wait_ge(bias_ready, 16 * 3)
            pe.wait_ge(prep_done, PREP_STEPS)

            def filter_in(i, c):
                if not exists(i, c):
                    return
                half = c % 2
                if half == 0:
                    pe.wait_ge(rbf_loaded[section_slot(c)], section_loads(i, c))
                if needed(group(i, c) - 1):
                    pe.wait_ge(ssp_done, group(i, c) - 1)
                nc.tensor.matmul(ps_z[:, c % 2, :], w_f1_sb[:, :],
                                 rbf_in[:, section_slot(c), half * GROUP:(half + 1) * GROUP],
                                 start=True, stop=True).then_inc(z_done, 1)

            def pick_rows(i, c, windows):
                if not exists(i, c):
                    return
                if windows:
                    if c % 2 == 0:
                        pe.wait_ge(win_loaded[section_slot(c)], section_loads(i, c))
                    pe.wait_ge(pick_done, group(i, c) + 1)
                else:
                    pe.wait_ge(gathered[c % 2], (i * (UNROLL // 2) + (c // 2 + 1)) * 16 * TILES_PER_GROUP)
                if needed(group(i, c) - 1):
                    pe.wait_ge(hcut_done, group(i, c) - 1)
                for q in range(TILES_PER_GROUP):
                    for t in range(PARTS):
                        if windows:
                            lhs, rhs = pick[:, c % 2, q * P:(q + 1) * P], h_win[:, section_slot(c), t, :]
                        else:
                            lhs, rhs = eye16[:, :], gath[:, c % 2, q, t * FEAT:(t + 1) * FEAT]
                        last = nc.tensor.matmul(ps_h[:, c % 2, q * FEAT:(q + 1) * FEAT], lhs, rhs,
                                                start=(t == 0), stop=(t == PARTS - 1))
                last.then_inc(hg_done, 1)

            def filter_out(i, c):
                if not exists(i, c):
                    return
                pe.wait_ge(ssp_done, group(i, c) + 1)
                if needed(group(i, c) - 1):
                    pe.wait_ge(msg_done, group(i, c) - 1)
                nc.tensor.matmul(ps_w[:, c % 2, :], ones16[:, 0:P], bias3[:, 0, :], start=True, stop=False)
                for q in range(TILES_PER_GROUP):
                    last = nc.tensor.matmul(ps_w[:, c % 2, q * FEAT:(q + 1) * FEAT],
                                            act1[:, c % 2, q * P:(q + 1) * P], w_f2_sb[:, :],
                                            start=False, stop=(q == TILES_PER_GROUP - 1))
                last.then_inc(w_done, 1)

            def merge(i, c):
                if not exists(i, c):
                    return
                pe.wait_ge(same_done, group(i, c) + 1)
                pe.wait_ge(msg_done, group(i, c) + 1)
                if needed(group(i, c)):
                    pe.wait_ge(copied, group(i, c))
                for q in range(TILES_PER_GROUP):
                    last = nc.tensor.matmul(ps_m[:, q // 2, (q % 2) * M:(q % 2 + 1) * M],
                                            same[:, c % 2, q * P:(q + 1) * P], msg[:, c % 2, q, :],
                                            start=True, stop=True)
                last.then_inc(merge_done, 1)

            def edge_step(windows):
                def step(i, c):
                    filter_in(i, c + 1)
                    filter_out(i, c)
                    merge(i, c - 1)
                    pick_rows(i, c + 1, windows)
                return step

            wide = pe.value_load(wide_flag[0:1, 0:1], min_val=0, max_val=1)
            with pe.If(wide < 1):
                over_edges(pe, edge_step(True), 1, 1)
            with pe.Else():
                over_edges(pe, edge_step(False), 1, 1)

            pe.wait_ge(msg_done, GROUPS)
            pe.wait_ge(hcut_done, GROUPS)

            def agg_transpose(i, c):
                if not there(i, c):
                    return
                b, slot = i * 2 + c, c % 2
                pe.wait_ge(agg_done, b + 1)
                if needed(b - 1):
                    pe.wait_ge(aggt_done, b - 1)
                for k in range(4):
                    last = nc.tensor.transpose(ps_z[:, slot, k * P:(k + 1) * P], agg[:, slot, k, :], eye_sb[:, :])
                last.then_inc(aggt_mm, 1)

            def out_first(i, c):
                if not there(i, c):
                    return
                b, slot = i * 2 + c, c % 2
                pe.wait_ge(aggt_done, b + 1)
                if needed(b - 1):
                    pe.wait_ge(ssp2_done, b - 1)
                nc.tensor.matmul(ps_w[:, slot, :], bias3[:, 1, 0:FEAT], ones16[:, :], start=True, stop=False)
                nc.tensor.matmul(ps_w[:, slot, :], w_o1_sb[:, :], agg_t[:, slot, :],
                                 start=False, stop=True).then_inc(z2_done, 1)

            def out_second(i, c):
                if not there(i, c):
                    return
                b, slot = i * 2 + c, c % 2
                pe.wait_ge(ssp2_done, b + 1)
                if needed(b - 1):
                    pe.wait_ge(res_done, b - 1)
                nc.tensor.matmul(ps_h[:, slot, :], ones16[:, 0:P], bias3[:, 2, :], start=True, stop=False)
                for k in range(4):
                    last = nc.tensor.matmul(ps_h[:, slot, k * FEAT:(k + 1) * FEAT],
                                            act1[:, slot, k * P:(k + 1) * P], w_o2_sb[:, :],
                                            start=False, stop=(k == 3))
                last.then_inc(o_done, 1)

            def out_step(i, c):
                out_first(i, c - 1)
                agg_transpose(i, c)
                out_second(i, c - 2)
            over_batches(pe, out_step, lag=3)

        @block.scalar
        def _(act):
            nc.scalar.preload_act_table_set("natural_log_exp_and_others")

            def h_first(i, c):
                if not there(i, c):
                    return
                b, slot = i * 2 + c, c % 2
                act.wait_ge(h_mm, b + 1)
                if needed(b - 1):
                    act.wait_ge(h_stored[slot], (i + c // 2) * 16)
                nc.scalar.copy(h_out[:, slot, :, 0, :],
                               ps_z[:, slot, :].rearrange("p (k f) -> p k f", k=4)).then_inc(h_hi, 1)

            def h_second(i, c):
                if not there(i, c):
                    return
                b, slot = i * 2 + c, c % 2
                act.wait_ge(h_r1, b + 1)
                nc.scalar.copy(h_out[:, slot, :, 1, :], h_rest[:, slot, :, :]).then_inc(h_mid, 1)

            def h_step(i, c):
                h_first(i, c)
                h_second(i, c - 1)
            over_batches(act, h_step, lag=1)
            act.wait_ge(col_in, 16 * COL_DMAS)
            act.wait_ge(prep_done, PREP_STEPS)

            def abs_step(i, c):
                if not exists(i, c):
                    return
                act.wait_ge(z_done, group(i, c) + 1)
                if needed(group(i, c) - 1):
                    act.wait_ge(ez_done, group(i, c) - 1)
                nc.scalar.activation(az[:, c % 2, :], ps_z[:, c % 2, :], ACT.Abs).then_inc(az_done, 1)

            def exp_step(i, c):
                if not exists(i, c):
                    return
                act.wait_ge(az_done, group(i, c) + 1)
                if needed(group(i, c) - 1):
                    act.wait_ge(y_done, group(i, c) - 1)
                nc.scalar.activation(ez[:, c % 2, :], az[:, c % 2, :], ACT.Exp, scale=-1.0).then_inc(ez_done, 1)

            def ln_step(i, c):
                if not exists(i, c):
                    return
                act.wait_ge(ez_done, group(i, c) + 1)
                if needed(group(i, c) - 1):
                    act.wait_ge(ssp_done, group(i, c) - 1)
                nc.scalar.activation(yz[:, c % 2, :], ez[:, c % 2, :], ACT.Ln, bias=half_sb[:, 0:1],
                                     scale=0.5).then_inc(y_done, 1)

            def cut_step(i, c):
                if not exists(i, c):
                    return
                act.wait_ge(hg_done, group(i, c) + 1)
                if needed(group(i, c) - 1):
                    act.wait_ge(msg_done, group(i, c) - 1)
                for q in range(TILES_PER_GROUP):
                    last = nc.scalar.activation(h_cut[:, c % 2, q, :], ps_h[:, c % 2, q * FEAT:(q + 1) * FEAT],
                                                ACT.Copy, scale=cut_sb[:, ds(group(i, c) * TILES_PER_GROUP + q, 1)])
                last.then_inc(hcut_done, 1)

            def copy_merged(i, c):
                if not exists(i, c):
                    return
                act.wait_ge(gap_done, group(i, c) + 1)
                back = c - MERGED_SLOTS
                for q in range(TILES_PER_GROUP):
                    if exists(i, back):
                        act.wait_ge(added[chain(back, q)], (chain_scatters(i, back, q) + 1) * 16)
                nc.scalar.copy(
                    merged[:, c % MERGED_SLOTS, :, :].rearrange("p (a b) f -> p a b f", a=2),
                    ps_m[:, :, 0:2 * M].rearrange("p a (b m) -> p a b m", m=M)[:, :, :, 0:FEAT]).then_inc(copied, 1)

            def edge_step(i, c):
                abs_step(i, c + 1)
                exp_step(i, c + 1)
                ln_step(i, c + 1)
                copy_merged(i, c - 1)
                cut_step(i, c + 1)
            over_edges(act, edge_step, 1, 1)

            def copy_agg(i, c):
                if not there(i, c):
                    return
                b, slot = i * 2 + c, c % 2
                act.wait_ge(aggt_mm, b + 1)
                if needed(b - 1):
                    act.wait_ge(z2_done, b - 1)
                nc.scalar.copy(agg_t[:, slot, :], ps_z[:, slot, :]).then_inc(aggt_done, 1)

            def out_ssp(i, c):
                if not there(i, c):
                    return
                b, slot = i * 2 + c, c % 2
                act.wait_ge(z2_done, b + 1)
                nc.scalar.activation(az[:, slot, :], ps_w[:, slot, :], ACT.Abs).then_inc(az2_done, 1)
                act.wait_ge(az2_done, b + 1)
                nc.scalar.activation(ez[:, slot, :], az[:, slot, :], ACT.Exp, scale=-1.0).then_inc(ez2_done, 1)
                act.wait_ge(ez2_done, b + 1)
                if needed(b - 1):
                    act.wait_ge(ssp2_done, b - 1)
                nc.scalar.activation(yz[:, slot, :], ez[:, slot, :], ACT.Ln, bias=half_sb[:, 0:1],
                                     scale=0.5).then_inc(y2_done, 1)

            def rstd_guess(i, c):
                if not there(i, c):
                    return
                b, slot = i * 2 + c, c % 2
                act.wait_ge(stat_done, b + 1)
                nc.scalar.activation(rstd[:, slot, 0, :], mean_var[:, slot, :, 1], ACT.Ln,
                                     bias=eps_sb[:, 0:1]).then_inc(ln_done, 1)
                act.wait_ge(ln_done, b + 1)
                if needed(b - 1):
                    act.wait_ge(shift_done, b - 1)
                nc.scalar.activation(rstd[:, slot, 1, :], rstd[:, slot, 0, :], ACT.Exp, scale=-0.5).then_inc(r0_done, 1)

            def normalise(i, c):
                if not there(i, c):
                    return
                b, slot = i * 2 + c, c % 2
                act.wait_ge(shift_done, b + 1)
                if needed(b - 1):
                    act.wait_ge(out_stored[slot], (i + c // 2) * 16)
                for k in range(4):
                    last = nc.scalar.activation(y_out[:, slot, k, :], res[:, slot, k, :], ACT.Identity,
                                                bias=rstd[:, slot, 4, k:k + 1], scale=rstd[:, slot, 3, k:k + 1])
                last.then_inc(norm_done, 1)

            def out_step(i, c):
                copy_agg(i, c)
                normalise(i, c - 3)
                out_ssp(i, c - 1)
                rstd_guess(i, c - 2)
            over_batches(act, out_step, lag=3)

        @block.vector
        def _(dve):
            nc.vector.memset(ones16[:, :], 1.0).then_inc(prep_done, 1)
            nc.vector.memset(half_sb[:, :], 0.5).then_inc(prep_done, 1)
            nc.vector.memset(eps_sb[:, :], EPS).then_inc(prep_done, 1)
            dve.wait_ge(row_in, 32)
            nc.vector.tensor_copy(row16[:, 0, :], row32[:, 0, :]).then_inc(idx_dve, 1)
            nc.vector.tensor_copy(row16[:, 1, :], row32[:, 1, :]).then_inc(idx_dve, 1)
            by_section = row32[:, 1, :].rearrange("p (a e) -> p a e", a=2)
            nc.vector.tensor_reduce(top_f[:, :], by_section, AX.X, ALU.max).then_inc(idx_dve, 1)
            nc.vector.tensor_reduce(base_f[:, :], by_section, AX.X, ALU.min).then_inc(idx_dve, 1)
            dve.wait_ge(idx_dve, 4)
            nc.vector.tensor_scalar(base_f[:, :], base_f[:, :], float(ROWS - P), None, ALU.min).then_inc(idx_dve, 1)
            dve.wait_ge(idx_dve, 5)
            nc.vector.tensor_tensor(span_f[:, :], top_f[:, :], base_f[:, :], ALU.subtract).then_inc(idx_dve, 1)
            dve.wait_ge(bias_in, 16 * 3)
            whole, rest = bias_row, bias_rest
            nc.vector.tensor_copy(bias_part[:, 0, :], whole).then_inc(bias_dve, 1)
            dve.wait_ge(bias_dve, 1)
            nc.vector.tensor_tensor(rest, whole, bias_part[:, 0, :], ALU.subtract).then_inc(bias_dve, 1)
            dve.wait_ge(bias_dve, 2)
            nc.vector.tensor_copy(bias_part[:, 1, :], rest).then_inc(bias_dve, 1)
            dve.wait_ge(bias_dve, 3)
            nc.vector.tensor_tensor(bias_part[:, 2, :], rest, bias_part[:, 1, :], ALU.subtract).then_inc(bias_dve, 1)
            dve.wait_ge(bias_dve, 4)

            def h_rest_1(i, c):
                if not there(i, c):
                    return
                b, slot = i * 2 + c, c % 2
                dve.wait_ge(h_hi, b + 1)
                nc.vector.tensor_tensor(h_rest[:, slot, :, :], ps_z[:, slot, :].rearrange("p (k f) -> p k f", k=4),
                                        h_out[:, slot, :, 0, :], ALU.subtract).then_inc(h_r1, 1)

            def h_rest_2(i, c):
                if not there(i, c):
                    return
                b, slot = i * 2 + c, c % 2
                dve.wait_ge(h_mid, b + 1)
                nc.vector.tensor_tensor(h_out[:, slot, :, 2, :], h_rest[:, slot, :, :], h_out[:, slot, :, 1, :],
                                        ALU.subtract).then_inc(h_lo, 1)

            def h_step(i, c):
                h_rest_1(i, c)
                h_rest_2(i, c - 1)
            over_batches(dve, h_step, lag=1)

            dve.wait_ge(const_in, 16 * CONST_DMAS)
            dve.wait_ge(col_in, 16 * COL_DMAS)
            nc.vector.tensor_copy(eye16[:, :], eye_sb[:, :]).then_inc(prep_done, 1)
            nc.vector.tensor_copy(msg[:, :, :, FEAT].rearrange("p a b -> p (a b)"),
                                  lane_sb[:, 2:3].to_broadcast([P, 8])).then_inc(prep_done, 1)
            nc.vector.tensor_copy(src_f[:, :], src_raw[:, :]).then_inc(prep_done, 1)
            nc.vector.tensor_scalar(spare_gap[:, :], src_raw[:, :], -1.0, lane_sb[:, 3:4],
                                    ALU.mult, ALU.add).then_inc(prep_done, 1)
            dve.wait_ge(base_in, 32)
            nc.vector.tensor_copy(base_reg[:, :], base_lane[0:1, :]).then_inc(prep_done, 1)
            nc.vector.tensor_reduce(span_max[:, :], span_row[:, :], AX.X, ALU.max).then_inc(prep_done, 1)
            dve.wait_ge(prep_done, 9)
            nc.vector.tensor_scalar(base_lane[:, :], base_lane[:, :], lane_sb[:, 0:1], None,
                                    ALU.add).then_inc(prep_done, 1)
            nc.vector.tensor_scalar(wide_flag[:, :], span_max[:, :], float(P), None, ALU.is_ge).then_inc(prep_done, 1)
            dve.wait_ge(prep_done, PREP_STEPS)

            def pick_step(i, c):
                if not exists(i, c):
                    return
                half = c % 2
                if half == 0:
                    dve.wait_ge(dst_loaded[section_slot(c)], section_loads(i, c))
                if needed(group(i, c) - 1):
                    dve.wait_ge(hg_done, group(i, c) - 1)
                nc.vector.tensor_scalar(pick[:, c % 2, :], dst_rep[:, section_slot(c), half * GROUP:(half + 1) * GROUP],
                                        base_lane[:, ds(section(i, c), 1)], None, ALU.is_equal).then_inc(pick_done, 1)

            def same_step(i, c):
                if not exists(i, c):
                    return
                half = c % 2
                if half == 0:
                    dve.wait_ge(src_loaded[section_slot(c)], section_loads(i, c))
                if needed(group(i, c) - 1):
                    dve.wait_ge(merge_done, group(i, c) - 1)
                nc.vector.tensor_tensor(
                    same[:, c % 2, :].rearrange("p (q e) -> p q e", q=4),
                    src_rep[:, section_slot(c), half * GROUP:(half + 1) * GROUP].rearrange("p (q e) -> p q e", q=4),
                    src_f[:, ds(group(i, c) * 4, 4)].unsqueeze(2).to_broadcast([P, 4, P]),
                    ALU.is_equal).then_inc(same_done, 1)

            def ssp_step(i, c):
                if not exists(i, c):
                    return
                dve.wait_ge(y_done, group(i, c) + 1)
                if needed(group(i, c) - 1):
                    dve.wait_ge(w_done, group(i, c) - 1)
                nc.vector.scalar_tensor_tensor(out=act1[:, c % 2, :], in0=ps_z[:, c % 2, :], scalar=0.0,
                                               in1=yz[:, c % 2, :], op0=ALU.max, op1=ALU.add).then_inc(ssp_done, 1)

            def msg_step(i, c):
                if not exists(i, c):
                    return
                dve.wait_ge(w_done, group(i, c) + 1)
                dve.wait_ge(hcut_done, group(i, c) + 1)
                if needed(group(i, c) - 1):
                    dve.wait_ge(merge_done, group(i, c) - 1)
                nc.vector.tensor_tensor(msg[:, c % 2, :, 0:FEAT], ps_w[:, c % 2, :].rearrange("p (q f) -> p q f", q=4),
                                        h_cut[:, c % 2, :, :], ALU.mult).then_inc(msg_done, 1)

            def idx_step(i, c):
                if not exists(i, c):
                    return
                dve.wait_ge(merge_done, group(i, c) + 1)
                nc.vector.scalar_tensor_tensor(
                    out=gap[:, c % MERGED_SLOTS, :].rearrange("p (a b) -> p a b", a=2),
                    in0=ps_m[:, :, 0:2 * M].rearrange("p a (b m) -> p a b m", m=M)[:, :, :, FEAT],
                    scalar=lane_sb[:, 1:2],
                    in1=spare_gap[:, ds(group(i, c) * TILES_PER_GROUP, TILES_PER_GROUP)].rearrange(
                        "p (a b) -> p a b", a=2),
                    op0=ALU.is_ge, op1=ALU.mult).then_inc(gap_done, 1)
                dve.wait_ge(gap_done, group(i, c) + 1)
                back = c - MERGED_SLOTS
                for q in range(TILES_PER_GROUP):
                    if exists(i, back):
                        dve.wait_ge(added[chain(back, q)], (chain_scatters(i, back, q) + 1) * 16)
                nc.vector.tensor_tensor(row_idx[:, c % MERGED_SLOTS, :], gap[:, c % MERGED_SLOTS, :],
                                        src_f[:, ds(group(i, c) * TILES_PER_GROUP, TILES_PER_GROUP)],
                                        ALU.add).then_inc(idx_done, 1)

            def edge_step(i, c):
                pick_step(i, c + 2)
                same_step(i, c)
                msg_step(i, c)
                idx_step(i, c - 1)
                ssp_step(i, c + 1)
            over_edges(dve, edge_step, 2, 1)

            def sum_parts(i, c):
                if not there(i, c):
                    return
                b, slot = i * 2 + c, c % 2
                dve.wait_ge(pair_sums, b + 1)
                nc.vector.tensor_tensor(acc_part[:, slot, 0, :], acc_part[:, slot, 0, :], acc_part[:, slot, 1, :],
                                        ALU.add).then_inc(part_sum, 1)

            def sum_all(i, c):
                if not there(i, c):
                    return
                b, slot = i * 2 + c, c % 2
                dve.wait_ge(part_sum, b + 1)
                if needed(b - 1):
                    dve.wait_ge(aggt_mm, b - 1)
                nc.vector.tensor_tensor(agg[:, slot, :, :].rearrange("p k f -> p (k f)"), acc_part[:, slot, 0, :],
                                        acc_part[:, slot, 2, :], ALU.add).then_inc(agg_done, 1)

            def out_ssp(i, c):
                if not there(i, c):
                    return
                b, slot = i * 2 + c, c % 2
                dve.wait_ge(y2_done, b + 1)
                if needed(b - 1):
                    dve.wait_ge(o_done, b - 1)
                nc.vector.scalar_tensor_tensor(out=act1[:, slot, :], in0=ps_w[:, slot, :], scalar=0.0,
                                               in1=yz[:, slot, :], op0=ALU.max, op1=ALU.add).then_inc(ssp2_done, 1)

            def residual(i, c):
                if not there(i, c):
                    return
                b, slot = i * 2 + c, c % 2
                dve.wait_ge(o_done, b + 1)
                dve.wait_ge(res_loaded[slot], (i + (c // 2 + 1)) * 16)
                if needed(b - 1):
                    dve.wait_ge(norm_done, b - 1)
                nc.vector.tensor_tensor(res[:, slot, :, :].rearrange("p k f -> p (k f)"), ps_h[:, slot, :],
                                        x_in[:, slot, :], ALU.add).then_inc(res_done, 1)
                dve.wait_ge(res_done, b + 1)
                for k in range(4):
                    last = nc.vector.bn_stats(stats[:, slot, k, :], res[:, slot, k, :])
                last.then_inc(var_done, 1)
                dve.wait_ge(var_done, b + 1)
                dve.nop(nofuse=True)
                for k in range(4):
                    last = nc.vector.bn_aggr(mean_var[:, slot, k, :], stats[:, slot, k, :])
                last.then_inc(stat_done, 1)

            def rstd_step(i, c):
                if not there(i, c):
                    return
                b, slot = i * 2 + c, c % 2
                r = [rstd[:, slot, k, :] for k in range(5)]
                dve.wait_ge(r0_done, b + 1)
                nc.vector.tensor_tensor(r[2], r[1], r[1], ALU.mult).then_inc(newton, 1)
                dve.wait_ge(newton, b * 4 + 1)
                nc.vector.scalar_tensor_tensor(out=r[3], in0=mean_var[:, slot, :, 1], scalar=EPS, in1=r[2],
                                               op0=ALU.add, op1=ALU.mult).then_inc(newton, 1)
                dve.wait_ge(newton, b * 4 + 2)
                nc.vector.tensor_scalar(r[4], r[3], -0.5, 1.5, ALU.mult, ALU.add).then_inc(newton, 1)
                dve.wait_ge(newton, b * 4 + 3)
                nc.vector.tensor_tensor(r[3], r[1], r[4], ALU.mult).then_inc(newton, 1)
                dve.wait_ge(newton, b * 4 + 4)
                nc.vector.scalar_tensor_tensor(out=r[4], in0=mean_var[:, slot, :, 0], scalar=-1.0, in1=r[3],
                                               op0=ALU.mult, op1=ALU.mult).then_inc(shift_done, 1)

            def out_step(i, c):
                rstd_step(i, c - 3)
                sum_parts(i, c)
                sum_all(i, c)
                out_ssp(i, c - 1)
                residual(i, c - 2)
            over_batches(dve, out_step, lag=3)


def kernel(x, src, dst, edge_attr3_1x20, edge_weight1, L0_gnn_W_in, L0_gnn_W_f1, L0_gnn_b_f1, L0_gnn_W_f2,
           L0_gnn_b_f2, L0_gnn_W_o1, L0_gnn_b_o1, L0_gnn_W_o2, L0_gnn_b_o2):
    import concourse.bacc as bacc
    from concourse.bass_utils import run_bass_kernel_spmd

    x, src, dst = np.asarray(x), np.asarray(src), np.asarray(dst)
    more_edges, more_rows = EDGE_ROWS - EDGES, ROWS - ATOMS
    x_rows = np.concatenate([x, np.zeros((more_rows, FEAT), x.dtype)])
    src_all = np.concatenate([src, np.full(more_edges, SPARE, src.dtype)])
    dst_all = np.concatenate([dst, np.full(more_edges, ATOMS - 1, dst.dtype)])
    cut = np.asarray(edge_weight1).reshape(EDGES)
    cut_all = np.concatenate([cut, np.zeros(more_edges, cut.dtype)])
    rbf = np.asarray(edge_attr3_1x20).reshape(EDGES, RBF)
    rbf_t = np.concatenate([np.concatenate([rbf.T, np.zeros((RBF, more_edges), rbf.dtype)], 1),
                            np.ones((1, EDGE_ROWS), rbf.dtype)])
    p = np.arange(P)
    lane = np.stack([p, 2.5 * 2.0 ** (60 - p), 2.0 ** (60 - p), SPARE + p], 1).astype(np.float32)

    def columns(v):
        return np.ascontiguousarray(v.reshape(TILES, P).T)

    arrays = {
        "x_rows": x_rows,
        "x_cols": np.ascontiguousarray(x_rows.reshape(BATCHES, P, 4, FEAT).transpose(3, 0, 2, 1).reshape(FEAT, ROWS)),
        "src_row": src_all.reshape(SECTIONS // 2, 2 * SECTION), "dst_row": dst_all.reshape(SECTIONS // 2, 2 * SECTION),
        "src_col": columns(src_all), "dst_col": columns(dst_all), "cut_col": columns(cut_all),
        "rbf_t": rbf_t,
        "w_in": np.asarray(L0_gnn_W_in), "w_f1": np.asarray(L0_gnn_W_f1),
        "b_f1": np.asarray(L0_gnn_b_f1).reshape(1, FEAT), "w_f2": np.asarray(L0_gnn_W_f2),
        "b_f2": np.asarray(L0_gnn_b_f2).reshape(1, FEAT), "w_o1": np.asarray(L0_gnn_W_o1),
        "b_o1": np.asarray(L0_gnn_b_o1).reshape(1, FEAT), "w_o2": np.asarray(L0_gnn_W_o2),
        "b_o2": np.asarray(L0_gnn_b_o2).reshape(1, FEAT),
        "lane": lane, "eye": np.eye(P, dtype=np.float32),
    }
    nc = bacc.Bacc("TRN2", target_bir_lowering=False, num_devices=1)
    args = [nc.dram_tensor(name, a.shape, mybir.dt.from_np(a.dtype), kind="ExternalInput").ap()
            for name, a in arrays.items()]
    out = nc.dram_tensor("out", (ATOMS, FEAT), mybir.dt.float32, kind="ExternalOutput").ap()
    gnn_program(nc, *args, out)
    result = run_bass_kernel_spmd(nc, [arrays], core_ids=[0])
    return result.results[0]["out"]
```

```python
import numpy as np
import concourse.bass as bass
from concourse import mybir
from contextlib import ExitStack

P = 128
ATOMS, FEAT, EDGES, RBF = 12500, 128, 212500, 20
TILES_PER_GROUP = 4
GROUP = TILES_PER_GROUP * P
SECTION = 2 * GROUP
SECTIONS = -(-EDGES // SECTION)
GROUPS = 2 * SECTIONS
TILES = GROUPS * TILES_PER_GROUP
REAL_TILES = -(-EDGES // P)
EDGE_ROWS = SECTIONS * SECTION
BATCH = 4 * P
BATCHES = -(-ATOMS // BATCH)
ROWS = BATCHES * BATCH
SPARE = ROWS - 2 * P
CHAINS = 4
FIRST_CHAINS, FIRST_GROUPS = 3, 9
UNROLL = 6
SECTION_SLOTS = 3
NODE_SLOTS = 4
CLEAR_BEFORE = 6
CLEAR_FROM, CLEAR_TO = 4, 9
ZERO_ROWS, LATE_ZERO_ROWS = 10, 5
PARTS = 3
MERGED_SLOTS = 3
EPS = 1e-5
assert SPARE >= ATOMS and SECTIONS % 2 == 0
assert FIRST_GROUPS * TILES_PER_GROUP % (FIRST_CHAINS * CHAINS) == 0
assert 0 <= TILES - REAL_TILES < TILES_PER_GROUP
assert UNROLL * TILES_PER_GROUP % CHAINS == 0 and UNROLL % (2 * SECTION_SLOTS) == 0 and UNROLL % MERGED_SLOTS == 0


def gnn_program(nc, x_rows, x_cols, src_row, dst_row, src_col, dst_col, cut_col, rbf_t,
                w_in, w_f1, b_f1, w_f2, b_f2, w_o1, b_o1, w_o2, b_o2, lane, eye, out):
    f32, bf16, i16, i32, u32 = (mybir.dt.float32, mybir.dt.bfloat16, mybir.dt.int16,
                                mybir.dt.int32, mybir.dt.uint32)
    ALU, ACT, AX = mybir.AluOpType, mybir.ActivationFunctionType, mybir.AxisListType
    ds = bass.ds
    ctx = ExitStack()
    with ctx:
        def sb(name, shape, dt):
            return ctx.enter_context(nc.sbuf_tensor(name, shape, dt))

        def sem(name):
            return ctx.enter_context(nc.semaphore(name))

        def sems(name, n):
            return [sem(f"{name}{k}") for k in range(n)]

        h_parts = nc.dram_tensor("h_parts", [ROWS, PARTS * FEAT], bf16).ap()
        src16 = nc.dram_tensor("src16", [SECTIONS, SECTION], i16).ap()
        dst16 = nc.dram_tensor("dst16", [SECTIONS, SECTION], i16).ap()
        base_dram = nc.dram_tensor("base_dram", [1, SECTIONS], f32).ap()
        span_dram = nc.dram_tensor("span_dram", [1, SECTIONS], f32).ap()
        accum = [nc.dram_tensor(f"accum{q}", [ROWS, FEAT], f32).ap() for q in range(CHAINS)]

        w_in_sb = sb("w_in_sb", [P, FEAT], f32)
        w_f1_sb = sb("w_f1_sb", [P, FEAT], f32)
        w_f2_sb = sb("w_f2_sb", [P, FEAT], f32)
        w_o1_sb = sb("w_o1_sb", [P, FEAT], f32)
        w_o2_sb = sb("w_o2_sb", [P, FEAT], f32)
        eye_sb = sb("eye_sb", [P, P], f32)
        eye16 = sb("eye16", [P, P], bf16)
        lane_sb = sb("lane_sb", [P, 4], f32)
        ones16 = sb("ones16", [P, GROUP], bf16)
        shared_a = sb("shared_a", [P, 3 * GROUP * 7 // 2], f32)
        bias_row = shared_a[0:1, 0:3 * GROUP]
        bias_rest = shared_a[0:1, 3 * GROUP:6 * GROUP]
        bias_part = shared_a[0:1, 6 * GROUP:].bitcast(bf16).rearrange("o (t e) -> o t e", t=PARTS)
        acc_part = shared_a[:, 0:2 * 2 * 4 * FEAT].rearrange("p (s n e) -> p s n e", s=2, n=2)
        bias3 = sb("bias3", [P, 3, GROUP], bf16)
        zero_rows = sb("zero_rows", [P, ZERO_ROWS, FEAT], f32)
        cut_sb = sb("cut_sb", [P, TILES], f32)
        src_raw = sb("src_raw", [P, TILES], i32)
        src_f = sb("src_f", [P, TILES], f32)
        spare_gap = sb("spare_gap", [P, TILES], f32)
        dst_idx = sb("dst_idx", [P, TILES], i32)
        base_lane = sb("base_lane", [P, SECTIONS], f32)
        base_reg = sb("base_reg", [1, SECTIONS], i32)
        span_row = sb("span_row", [1, SECTIONS], f32)
        span_max = sb("span_max", [1, 1], f32)
        wide_flag = sb("wide_flag", [1, 1], i32)
        HALF = SECTIONS // 2
        shared_b = sb("shared_b", [P, NODE_SLOTS * CHAINS * 4 * FEAT], f32)
        row32 = shared_b[0:HALF, 0:4 * SECTION].bitcast(i32).rearrange("p (a e) -> p a e", a=2)
        row16 = shared_b[0:HALF, 4 * SECTION:6 * SECTION].bitcast(i16).rearrange("p (a e) -> p a e", a=2)
        acc_in = shared_b[:, :].rearrange("p (s q e) -> p s q e", s=NODE_SLOTS, q=CHAINS)
        base_f = sb("base_f", [HALF, 2], f32)
        top_f = sb("top_f", [HALF, 2], f32)
        span_f = sb("span_f", [HALF, 2], f32)

        rbf_in = sb("rbf_in", [P, SECTION_SLOTS, SECTION], f32)
        src_rep = sb("src_rep", [P, SECTION_SLOTS, SECTION], i16)
        dst_rep = sb("dst_rep", [P, SECTION_SLOTS, SECTION], i16)
        h_win = sb("h_win", [P, SECTION_SLOTS, PARTS, FEAT], bf16)
        pick = sb("pick", [P, 2, GROUP], bf16)
        same = sb("same", [P, 2, GROUP], f32)
        az = sb("az", [P, 2, GROUP], f32)
        ez = sb("ez", [P, 2, GROUP], f32)
        yz = sb("yz", [P, 2, GROUP], f32)
        act1 = sb("act1", [P, 2, GROUP], f32)
        h_cut = sb("h_cut", [P, 2, TILES_PER_GROUP, FEAT], f32)
        msg = sb("msg", [P, 2, TILES_PER_GROUP, FEAT + 1], f32)
        merged = sb("merged", [P, MERGED_SLOTS, TILES_PER_GROUP, FEAT], f32)
        gap = sb("gap", [P, MERGED_SLOTS, TILES_PER_GROUP], f32)
        row_idx = sb("row_idx", [P, MERGED_SLOTS, TILES_PER_GROUP], i32)
        gath_idx = sb("gath_idx", [P, 2, TILES_PER_GROUP], i32)
        gath = sb("gath", [P, 2, TILES_PER_GROUP, PARTS * FEAT], bf16)

        x_in = sb("x_in", [P, NODE_SLOTS, BATCH], f32)
        h_out = sb("h_out", [P, NODE_SLOTS, 4, PARTS, FEAT], bf16)
        h_rest = sb("h_rest", [P, NODE_SLOTS, 4, FEAT], f32)
        agg, agg_t = h_cut, same
        res = sb("res", [P, NODE_SLOTS, 4, FEAT], f32)
        stats = sb("stats", [P, NODE_SLOTS, 4, 6], f32)
        mean_var = sb("mean_var", [P, NODE_SLOTS, 4, 2], f32)
        rstd = sb("rstd", [P, NODE_SLOTS, 5, 4], f32)
        y_out = h_rest
        eps_sb = sb("eps_sb", [P, 1], f32)
        half_sb = sb("half_sb", [P, 1], f32)

        ps_z = ctx.enter_context(nc.psum_tensor("ps_z", [P, 2, GROUP], f32))
        ps_w = ctx.enter_context(nc.psum_tensor("ps_w", [P, 2, GROUP], f32))
        ps_h = ctx.enter_context(nc.psum_tensor("ps_h", [P, 2, GROUP], f32))
        ps_m = ctx.enter_context(nc.psum_tensor("ps_m", [P, 2, GROUP], f32))
        ps_hx = [ps_z[:, 0, :], ps_z[:, 1, :], ps_w[:, 0, :], ps_w[:, 1, :]]
        M = FEAT + 1

        const_in, bias_in, bias_dve, bias_ready = sem("const_in"), sem("bias_in"), sem("bias_dve"), sem("bias_ready")
        col_in, row_in, dst_in, idx_dve = sem("col_in"), sem("row_in"), sem("dst_in"), sem("idx_dve")
        row_out, base_out, base_in, prep_done = sem("row_out"), sem("base_out"), sem("base_in"), sem("prep_done")
        zero_set, zeroed = sem("zero_set"), sems("zeroed", CHAINS)
        w_in_loaded, padded = sem("w_in_loaded"), sem("padded")
        x_loaded = sems("x_loaded", NODE_SLOTS)
        h_mm, h_hi, h_r1, h_mid, h_lo = (sem(n) for n in ("h_mm", "h_hi", "h_r1", "h_mid", "h_lo"))
        h_stored = sems("h_stored", NODE_SLOTS)
        rbf_loaded, src_loaded = sems("rbf_loaded", SECTION_SLOTS), sems("src_loaded", SECTION_SLOTS)
        dst_loaded, win_loaded = sems("dst_loaded", SECTION_SLOTS), sems("win_loaded", SECTION_SLOTS)
        gathered = sems("gathered", 2)
        (z_done, ez_done, y_done, ssp_done, pick_done, same_done, hg_done, hcut_done, w_done, msg_done,
         merge_done, copied, gap_done, idx_done) = (
            sem(n) for n in ("z_done", "ez_done", "y_done", "ssp_done", "pick_done", "same_done", "hg_done",
                             "hcut_done", "w_done", "msg_done", "merge_done", "copied", "gap_done", "idx_done"))
        gath_listed = sem("gath_listed")
        az_done, az2_done = sem("az_done"), sem("az2_done")
        added = sems("added", CHAINS)
        acc_loaded, res_loaded, out_stored = sems("acc_loaded", NODE_SLOTS), sems("res_loaded", NODE_SLOTS), sems("out_stored", NODE_SLOTS)
        (pair_sums, agg_done, aggt_mm, aggt_done, z2_done, ez2_done, y2_done, ssp2_done, o_done, res_done,
         stat_done, var_done, ln_done, r0_done, newton, shift_done, norm_done) = (
            sem(n) for n in ("pair_sums", "agg_done", "aggt_mm", "aggt_done", "z2_done", "ez2_done", "y2_done",
                             "ssp2_done", "o_done", "res_done", "stat_done", "var_done", "ln_done", "r0_done",
                             "newton", "shift_done", "norm_done"))
        CONST_DMAS, COL_DMAS, PREP_STEPS = 7, 2, 11

        def group(i, c):
            return i * UNROLL + c

        def section(i, c):
            return i * (UNROLL // 2) + c // 2

        def section_slot(c):
            return c // 2 % SECTION_SLOTS

        def section_loads(i, c):
            return (i * (UNROLL // 2 // SECTION_SLOTS) + (c // 2 // SECTION_SLOTS + 1)) * 16

        FIRST_TILES = FIRST_GROUPS * TILES_PER_GROUP

        def chain(i, c, q):
            first = isinstance(i, int) and group(i, c) < FIRST_GROUPS
            return (c * TILES_PER_GROUP + q) % (FIRST_CHAINS if first else CHAINS)

        def chain_scatters(i, c, q):
            if isinstance(i, int) and group(i, c) < FIRST_GROUPS:
                return (group(i, c) * TILES_PER_GROUP + q) // FIRST_CHAINS
            more = FIRST_TILES // FIRST_CHAINS if chain(i, c, q) < FIRST_CHAINS else 0
            return i * (UNROLL * TILES_PER_GROUP // CHAINS) + (
                (c * TILES_PER_GROUP + q) // CHAINS + more - FIRST_TILES // CHAINS)

        def scatters_in_all(k):
            return len(range(k, FIRST_TILES, FIRST_CHAINS)) * (k < FIRST_CHAINS) + len(range(FIRST_TILES + k, REAL_TILES, CHAINS))

        def exists(i, c):
            return not isinstance(i, int) or 0 <= UNROLL * i + c < GROUPS

        def there(i, c):
            return not isinstance(i, int) or 0 <= NODE_SLOTS * i + c < BATCHES

        def slot_dmas(i, c):
            return (i + (c // NODE_SLOTS + 1)) * 16

        def dmas_in_all(slot):
            return 16 * len(range(slot, BATCHES, NODE_SLOTS))

        def needed(value):
            return not isinstance(value, int) or value > 0

        def pipeline(engine, step, count, unroll, lead, lag, peeled=0):
            first, last = max(-(-(lag + 3) // unroll), peeled), (count - lead) // unroll
            for c in range(-lead, unroll * first):
                step(0, c)
            with engine.Fori(first, last) as i:
                for c in range(unroll):
                    step(i, c)
            for c in range(count - unroll * last + lag):
                step(last, c)

        def over_edges(engine, step, lead, lag):
            peeled = -(-(FIRST_GROUPS + lag + MERGED_SLOTS) // UNROLL)
            pipeline(engine, step, GROUPS, UNROLL, lead, lag, peeled)

        def over_batches(engine, step, lead=0, lag=0):
            pipeline(engine, step, BATCHES, NODE_SLOTS, lead, lag)

        block = ctx.enter_context(nc.Block())

        @block.sync
        def _(sp):
            def h_load(i, c):
                if not there(i, c):
                    return
                b = i * NODE_SLOTS + c
                if needed(b - NODE_SLOTS + 1):
                    sp.wait_ge(h_mm, b - NODE_SLOTS + 1)
                    sp.nop(nofuse=True)
                sp.dma_start(x_in[:, c % NODE_SLOTS, :], x_cols[:, ds(b * BATCH, BATCH)]).then_inc(
                    x_loaded[c % NODE_SLOTS], 16)

            def h_store(i, c):
                if not there(i, c):
                    return
                b = i * NODE_SLOTS + c
                sp.wait_ge(h_lo, b + 1)
                sp.nop(nofuse=True)
                sp.dma_start(h_parts[ds(b * BATCH, BATCH), :].rearrange("(p k) f -> p (k f)", k=4),
                             h_out[:, c % NODE_SLOTS, :, :, :].rearrange("p k t f -> p (k t f)")).then_inc(
                    h_stored[c % NODE_SLOTS], 16)

            def h_step(i, c):
                h_load(i, c + 3)
                h_store(i, c - 1)

            sp.dma_start(w_in_sb[:, :], w_in).then_inc(w_in_loaded, 16)
            over_batches(sp, h_step, lead=3, lag=1)
            sp.wait_ge(row_out, 32)
            sp.wait_ge(prep_done, PREP_STEPS)

            def load_section(i, c, windows):
                slot, before = section_slot(c), group(i, c) - 2 * SECTION_SLOTS + 2
                if windows:
                    first = sp.value_load(base_reg[0:1, ds(section(i, c), 1)], min_val=0, max_val=ROWS - P)
                if needed(before):
                    sp.wait_ge(z_done, before)
                    sp.nop(nofuse=True)
                sp.dma_start(rbf_in[0:RBF + 1, slot, :], rbf_t[:, ds(section(i, c) * SECTION, SECTION)]).then_inc(
                    rbf_loaded[slot], 16)
                if needed(before):
                    sp.wait_ge(pick_done, before)
                    sp.nop(nofuse=True)
                sp.dma_start(dst_rep[:, slot, :], dst16[ds(section(i, c), 1), :].to_broadcast([P, SECTION])).then_inc(
                    dst_loaded[slot], 16)
                if windows:
                    if needed(before):
                        sp.wait_ge(hg_done, before)
                        sp.nop(nofuse=True)
                    if isinstance(i, int) and group(i, c) == 0:
                        for k in range(NODE_SLOTS):
                            sp.wait_ge(h_stored[k], dmas_in_all(k))
                    sp.dma_start(h_win[:, slot, :, :].rearrange("p t f -> p (t f)"),
                                 h_parts[ds(first, P), :]).then_inc(win_loaded[slot], 16)
                if needed(before):
                    sp.wait_ge(same_done, before)
                    sp.nop(nofuse=True)
                sp.dma_start(src_rep[:, slot, :], src16[ds(section(i, c), 1), :].to_broadcast([P, SECTION])).then_inc(
                    src_loaded[slot], 16)

            def load_all(windows):
                def step(i, c):
                    if exists(i, c) and c % 2 == 0:
                        load_section(i, c, windows)
                over_edges(sp, step, 0, 0)

            sp.wait_ge(padded, 3)
            wide = sp.value_load(wide_flag[0:1, 0:1], min_val=0, max_val=1)
            with sp.If(wide < 1):
                load_all(True)
            with sp.Else():
                load_all(False)

            def res_load(i, c):
                if not there(i, c):
                    return
                b = i * NODE_SLOTS + c
                if needed(b - NODE_SLOTS + 1):
                    sp.wait_ge(res_done, b - NODE_SLOTS + 1)
                    sp.nop(nofuse=True)
                sp.dma_start(x_in[:, c % NODE_SLOTS, :],
                             x_rows[ds(b * BATCH, BATCH), :].rearrange("(p k) f -> p (k f)", k=4)).then_inc(
                    res_loaded[c % NODE_SLOTS], 16)

            for b in range(NODE_SLOTS):
                res_load(0, b)
            for q in range(CHAINS):
                sp.wait_ge(added[q], 16 * scatters_in_all(q))

            def acc_load(i, c):
                if not there(i, c):
                    return
                b = i * NODE_SLOTS + c
                if needed(b - NODE_SLOTS + 1):
                    sp.wait_ge(pair_sums, b - NODE_SLOTS + 1)
                    sp.nop(nofuse=True)
                for q in range(CHAINS):
                    sp.dma_start(acc_in[:, c % NODE_SLOTS, q, :],
                                 accum[q][ds(b * BATCH, BATCH), :].rearrange("(p k) f -> p (k f)", k=4)).then_inc(
                        acc_loaded[c % NODE_SLOTS], 16)

            def out_store(i, c):
                if not there(i, c):
                    return
                b = i * NODE_SLOTS + c
                sp.wait_ge(norm_done, b + 1)
                sp.nop(nofuse=True)
                rows = BATCH
                if isinstance(i, int) and b == BATCHES - 1:
                    rows = ATOMS - b * BATCH
                sp.dma_start(out[ds(b * BATCH, rows), :].rearrange("(p k) f -> p (k f)", k=4),
                             y_out[0:rows // 4, c % NODE_SLOTS, :, :].rearrange("p k f -> p (k f)")).then_inc(
                    out_stored[c % NODE_SLOTS], 16)

            def out_step(i, c):
                acc_load(i, c + 3)
                if not isinstance(i, int) or i * NODE_SLOTS + c >= NODE_SLOTS:
                    res_load(i, c)
                out_store(i, c - 6)
            over_batches(sp, out_step, lead=3, lag=6)
            for slot in range(NODE_SLOTS):
                sp.wait_ge(out_stored[slot], dmas_in_all(slot))

        @block.gpsimd
        def _(pool):
            nc.gpsimd.memset(w_f1_sb[:, :], 0.0).then_inc(padded, 1)
            nc.gpsimd.memset(bias3[:, :, :], 0.0).then_inc(padded, 1)
            nc.gpsimd.memset(zero_rows[:, :, :], 0.0).then_inc(zero_set, 1)
            nc.gpsimd.memset(rbf_in[:, :, :], 0.0).then_inc(padded, 1)
            rows_each = ROWS // P
            pool.wait_ge(zero_set, 1)

            def clear_first(pieces):
                for n in pieces:
                    q, r = n % FIRST_CHAINS, n // FIRST_CHAINS * ZERO_ROWS
                    if n >= 2:
                        pool.wait_ge(zeroed[(n - 2) % FIRST_CHAINS], ((n - 2) // FIRST_CHAINS + 1) * 16)
                    pool.dma_start(accum[q].rearrange("(p r) f -> p r f", r=rows_each)[:, r:r + ZERO_ROWS, :],
                                   zero_rows[:, :, :]).then_inc(zeroed[q], 16)

            clear_first(range(CLEAR_BEFORE))
            pool.wait_ge(idx_dve, 2)
            pool.dma_start(src16.rearrange("(p a) e -> p (a e)", a=2), row16[:, 0, :]).then_inc(row_out, 16)
            pool.dma_start(dst16.rearrange("(p a) e -> p (a e)", a=2), row16[:, 1, :]).then_inc(row_out, 16)
            pool.wait_ge(idx_dve, 6)
            pool.dma_start(base_dram.rearrange("o (p a) -> (o p) a", a=2), base_f[:, :]).then_inc(base_out, 16)
            pool.dma_start(span_dram.rearrange("o (p a) -> (o p) a", a=2), span_f[:, :]).then_inc(base_out, 16)
            pool.wait_ge(bias_dve, 4)
            for t in range(PARTS):
                pool.dma_start(bias3[t:t + 1, :, :].rearrange("o b e -> o (b e)"),
                               bias_part[:, t, :]).then_inc(bias_ready, 16)
            pool.wait_ge(base_out, 32)
            pool.dma_start(span_row[:, :], span_dram).then_inc(base_in, 16)
            pool.dma_start(base_lane[:, :], base_dram.to_broadcast([P, SECTIONS])).then_inc(base_in, 16)
            clear_first(range(CLEAR_BEFORE, FIRST_CHAINS * (rows_each // ZERO_ROWS)))
            pool.wait_ge(prep_done, PREP_STEPS)
            for slot in range(NODE_SLOTS):
                pool.wait_ge(h_stored[slot], dmas_in_all(slot))

            def scatter(i, c):
                if not exists(i, c):
                    return
                pool.wait_ge(copied, group(i, c) + 1)
                pool.wait_ge(idx_done, group(i, c) + 1)
                for q in range(TILES_PER_GROUP):
                    if isinstance(i, int) and group(i, c) * TILES_PER_GROUP + q >= REAL_TILES:
                        continue
                    k = chain(i, c, q)
                    if needed(chain_scatters(i, c, q)):
                        pool.wait_ge(added[k], chain_scatters(i, c, q) * 16)
                        pool.nop(nofuse=True)
                    else:
                        rows = ZERO_ROWS if k < FIRST_CHAINS else LATE_ZERO_ROWS
                        pool.wait_ge(zeroed[k], 16 * (ROWS // P // rows))
                    nc.gpsimd.indirect_dma_start(
                        out=accum[k],
                        out_offset=bass.IndirectOffsetOnAxis(
                            ap=row_idx[:, c % MERGED_SLOTS, q:q + 1].bitcast(u32), axis=0),
                        in_=merged[:, c % MERGED_SLOTS, q, :], in_offset=None,
                        compute_op=ALU.add).then_inc(added[k], 16)

            def gather(i, c):
                if not exists(i, c):
                    return
                if needed(group(i, c) - 1):
                    pool.wait_ge(hg_done, group(i, c) - 1)
                nc.gpsimd.tensor_copy(gath_idx[:, c % 2, :], dst_idx[:, ds(group(i, c) * 4, 4)]).then_inc(gath_listed, 1)
                pool.wait_ge(gath_listed, group(i, c) + 1)
                pool.nop(nofuse=True)
                for q in range(TILES_PER_GROUP):
                    nc.gpsimd.indirect_dma_start(
                        out=gath[:, c % 2, q, :], out_offset=None, in_=h_parts,
                        in_offset=bass.IndirectOffsetOnAxis(
                            ap=gath_idx[:, c % 2, q:q + 1].bitcast(u32), axis=0),
                    ).then_inc(gathered[c % 2], 16)

            def general(i, c):
                gather(i, c + 2)
                scatter(i, c)

            wide = pool.value_load(wide_flag[0:1, 0:1], min_val=0, max_val=1)
            with pool.If(wide < 1):
                over_edges(pool, scatter, 0, 0)
            with pool.Else():
                pool.dma_start(dst_idx[:, :], dst_col).then_inc(dst_in, 16)
                pool.wait_ge(dst_in, 16)
                over_edges(pool, general, 2, 0)

            def add_pairs(i, c):
                if not there(i, c):
                    return
                b, slot = i * NODE_SLOTS + c, c % 2
                pool.wait_ge(acc_loaded[c % NODE_SLOTS], slot_dmas(i, c) * CHAINS)
                if needed(b - 1):
                    pool.wait_ge(agg_done, b - 1)
                for k in range(CHAINS // 2):
                    last = nc.gpsimd.tensor_tensor(acc_part[:, slot, k, :], acc_in[:, c % NODE_SLOTS, 2 * k, :],
                                                   acc_in[:, c % NODE_SLOTS, 2 * k + 1, :], ALU.add)
                last.then_inc(pair_sums, 1)
            over_batches(pool, add_pairs)

        @block.tensor
        def _(pe):
            pe.wait_ge(w_in_loaded, 16)

            def h_product(i, c):
                if not there(i, c):
                    return
                b, slot = i * NODE_SLOTS + c, c % NODE_SLOTS
                pe.wait_ge(x_loaded[slot], slot_dmas(i, c))
                if needed(b - NODE_SLOTS + 1):
                    pe.wait_ge(h_r1, b - NODE_SLOTS + 1)
                for k in range(4):
                    last = nc.tensor.matmul(ps_hx[slot][:, k * FEAT:(k + 1) * FEAT],
                                            x_in[:, slot, k * P:(k + 1) * P], w_in_sb[:, :], start=True, stop=True)
                last.then_inc(h_mm, 1)
            over_batches(pe, h_product)
            pe.wait_ge(h_r1, BATCHES)
            pe.wait_ge(const_in, 16 * CONST_DMAS)
            pe.wait_ge(bias_ready, 16 * 3)
            pe.wait_ge(prep_done, PREP_STEPS)

            def filter_in(i, c):
                if not exists(i, c):
                    return
                half = c % 2
                if half == 0:
                    pe.wait_ge(rbf_loaded[section_slot(c)], section_loads(i, c))
                if needed(group(i, c) - 1):
                    pe.wait_ge(ssp_done, group(i, c) - 1)
                nc.tensor.matmul(ps_z[:, c % 2, :], w_f1_sb[:, :],
                                 rbf_in[:, section_slot(c), half * GROUP:(half + 1) * GROUP],
                                 start=True, stop=True).then_inc(z_done, 1)

            def pick_rows(i, c, windows):
                if not exists(i, c):
                    return
                if windows:
                    if c % 2 == 0:
                        pe.wait_ge(win_loaded[section_slot(c)], section_loads(i, c))
                else:
                    pe.wait_ge(gathered[c % 2], (i * (UNROLL // 2) + (c // 2 + 1)) * 16 * TILES_PER_GROUP)
                pe.wait_ge(pick_done, group(i, c) + 1)
                if needed(group(i, c) - 1):
                    pe.wait_ge(hcut_done, group(i, c) - 1)
                for q in range(TILES_PER_GROUP):
                    for t in range(PARTS):
                        if windows:
                            lhs, rhs = pick[:, c % 2, q * P:(q + 1) * P], h_win[:, section_slot(c), t, :]
                        else:
                            lhs, rhs = eye16[:, :], gath[:, c % 2, q, t * FEAT:(t + 1) * FEAT]
                        last = nc.tensor.matmul(ps_h[:, c % 2, q * FEAT:(q + 1) * FEAT], lhs, rhs,
                                                start=(t == 0), stop=(t == PARTS - 1))
                last.then_inc(hg_done, 1)

            def filter_out(i, c):
                if not exists(i, c):
                    return
                pe.wait_ge(ssp_done, group(i, c) + 1)
                if needed(group(i, c) - 1):
                    pe.wait_ge(msg_done, group(i, c) - 1)
                nc.tensor.matmul(ps_w[:, c % 2, :], ones16[:, 0:P], bias3[:, 0, :], start=True, stop=False)
                for q in range(TILES_PER_GROUP):
                    last = nc.tensor.matmul(ps_w[:, c % 2, q * FEAT:(q + 1) * FEAT],
                                            act1[:, c % 2, q * P:(q + 1) * P], w_f2_sb[:, :],
                                            start=False, stop=(q == TILES_PER_GROUP - 1))
                last.then_inc(w_done, 1)

            def merge(i, c):
                if not exists(i, c):
                    return
                pe.wait_ge(same_done, group(i, c) + 1)
                pe.wait_ge(msg_done, group(i, c) + 1)
                if needed(group(i, c)):
                    pe.wait_ge(copied, group(i, c))
                for q in range(TILES_PER_GROUP):
                    last = nc.tensor.matmul(ps_m[:, q // 2, (q % 2) * M:(q % 2 + 1) * M],
                                            same[:, c % 2, q * P:(q + 1) * P], msg[:, c % 2, q, :],
                                            start=True, stop=True)
                last.then_inc(merge_done, 1)

            def edge_step(windows):
                def step(i, c):
                    filter_in(i, c + 1)
                    filter_out(i, c)
                    merge(i, c - 1)
                    pick_rows(i, c + 1, windows)
                return step

            wide = pe.value_load(wide_flag[0:1, 0:1], min_val=0, max_val=1)
            with pe.If(wide < 1):
                over_edges(pe, edge_step(True), 1, 1)
            with pe.Else():
                over_edges(pe, edge_step(False), 1, 1)

            pe.wait_ge(msg_done, GROUPS)
            pe.wait_ge(hcut_done, GROUPS)

            def agg_transpose(i, c):
                if not there(i, c):
                    return
                b, slot = i * NODE_SLOTS + c, c % 2
                pe.wait_ge(agg_done, b + 1)
                if needed(b - 1):
                    pe.wait_ge(aggt_done, b - 1)
                for k in range(4):
                    last = nc.tensor.transpose(ps_z[:, slot, k * P:(k + 1) * P], agg[:, slot, k, :], eye_sb[:, :])
                last.then_inc(aggt_mm, 1)

            def out_first(i, c):
                if not there(i, c):
                    return
                b, slot = i * NODE_SLOTS + c, c % 2
                pe.wait_ge(aggt_done, b + 1)
                if needed(b - 1):
                    pe.wait_ge(ssp2_done, b - 1)
                nc.tensor.matmul(ps_w[:, slot, :], bias3[:, 1, 0:FEAT], ones16[:, :], start=True, stop=False)
                nc.tensor.matmul(ps_w[:, slot, :], w_o1_sb[:, :], agg_t[:, slot, :],
                                 start=False, stop=True).then_inc(z2_done, 1)

            def out_second(i, c):
                if not there(i, c):
                    return
                b, slot = i * NODE_SLOTS + c, c % 2
                pe.wait_ge(ssp2_done, b + 1)
                if needed(b - 1):
                    pe.wait_ge(res_done, b - 1)
                nc.tensor.matmul(ps_h[:, slot, :], ones16[:, 0:P], bias3[:, 2, :], start=True, stop=False)
                for k in range(4):
                    last = nc.tensor.matmul(ps_h[:, slot, k * FEAT:(k + 1) * FEAT],
                                            act1[:, slot, k * P:(k + 1) * P], w_o2_sb[:, :],
                                            start=False, stop=(k == 3))
                last.then_inc(o_done, 1)

            def out_step(i, c):
                agg_transpose(i, c)
                out_first(i, c - 1)
                out_second(i, c - 2)
            over_batches(pe, out_step, lag=2)

        @block.scalar
        def _(act):
            nc.scalar.preload_act_table_set("natural_log_exp_and_others")
            act.dma_start(row32[:, 0, :], src_row).then_inc(row_in, 16)
            act.dma_start(row32[:, 1, :], dst_row).then_inc(row_in, 16)
            act.dma_start(lane_sb[:, :], lane).then_inc(const_in, 16)
            for k, b in enumerate((b_f2, b_o1, b_o2)):
                act.dma_start(bias_row[:, k * GROUP:(k + 1) * GROUP].rearrange("o (r f) -> o r f", r=4),
                              b.unsqueeze(1).to_broadcast([1, 4, FEAT])).then_inc(bias_in, 16)
            act.dma_start(eye_sb[:, :], eye).then_inc(const_in, 16)
            act.dma_start(src_raw[:, :], src_col).then_inc(col_in, 16)
            act.dma_start(cut_sb[:, :], cut_col).then_inc(col_in, 16)
            act.wait_ge(padded, 2)
            act.dma_start(w_f1_sb[0:RBF, :], w_f1).then_inc(const_in, 16)
            act.dma_start(w_f1_sb[RBF:RBF + 1, :], b_f1).then_inc(const_in, 16)
            act.dma_start(w_f2_sb[:, :], w_f2).then_inc(const_in, 16)
            act.dma_start(w_o1_sb[:, :], w_o1).then_inc(const_in, 16)
            act.dma_start(w_o2_sb[:, :], w_o2).then_inc(const_in, 16)

            def h_first(i, c):
                if not there(i, c):
                    return
                b, slot = i * NODE_SLOTS + c, c % NODE_SLOTS
                act.wait_ge(h_mm, b + 1)
                if needed(b - NODE_SLOTS + 1):
                    act.wait_ge(h_stored[slot], slot_dmas(i, c) - 16)
                nc.scalar.copy(h_out[:, slot, :, 0, :],
                               ps_hx[slot].rearrange("p (k f) -> p k f", k=4)).then_inc(h_hi, 1)

            def h_second(i, c):
                if not there(i, c):
                    return
                b, slot = i * NODE_SLOTS + c, c % NODE_SLOTS
                act.wait_ge(h_r1, b + 1)
                nc.scalar.copy(h_out[:, slot, :, 1, :], h_rest[:, slot, :, :]).then_inc(h_mid, 1)

            def h_step(i, c):
                h_first(i, c)
                h_second(i, c - 1)
            over_batches(act, h_step, lag=1)
            act.wait_ge(zero_set, 1)
            act.wait_ge(col_in, 16 * COL_DMAS)
            act.wait_ge(prep_done, PREP_STEPS)

            def clear_step(i, c):
                if not isinstance(i, int) or not CLEAR_FROM <= group(i, c) < CLEAR_TO:
                    return
                pieces = [(q, r) for q in range(FIRST_CHAINS, CHAINS) for r in range(0, ROWS // P, LATE_ZERO_ROWS)]
                each = -(-len(pieces) // (CLEAR_TO - CLEAR_FROM))
                for q, r in pieces[each * (group(i, c) - CLEAR_FROM):each * (group(i, c) - CLEAR_FROM + 1)]:
                    act.dma_start(accum[q].rearrange("(p r) f -> p r f", r=ROWS // P)[:, r:r + LATE_ZERO_ROWS, :],
                                  zero_rows[:, 0:LATE_ZERO_ROWS, :]).then_inc(zeroed[q], 16)

            def abs_step(i, c):
                if not exists(i, c):
                    return
                act.wait_ge(z_done, group(i, c) + 1)
                if needed(group(i, c) - 1):
                    act.wait_ge(ez_done, group(i, c) - 1)
                nc.scalar.activation(az[:, c % 2, :], ps_z[:, c % 2, :], ACT.Abs).then_inc(az_done, 1)

            def exp_step(i, c):
                if not exists(i, c):
                    return
                act.wait_ge(az_done, group(i, c) + 1)
                if needed(group(i, c) - 1):
                    act.wait_ge(y_done, group(i, c) - 1)
                nc.scalar.activation(ez[:, c % 2, :], az[:, c % 2, :], ACT.Exp, scale=-1.0).then_inc(ez_done, 1)

            def ln_step(i, c):
                if not exists(i, c):
                    return
                act.wait_ge(ez_done, group(i, c) + 1)
                if needed(group(i, c) - 1):
                    act.wait_ge(ssp_done, group(i, c) - 1)
                nc.scalar.activation(yz[:, c % 2, :], ez[:, c % 2, :], ACT.Ln, bias=half_sb[:, 0:1],
                                     scale=0.5).then_inc(y_done, 1)

            def cut_step(i, c):
                if not exists(i, c):
                    return
                act.wait_ge(hg_done, group(i, c) + 1)
                if needed(group(i, c) - 1):
                    act.wait_ge(msg_done, group(i, c) - 1)
                for q in range(TILES_PER_GROUP):
                    last = nc.scalar.activation(h_cut[:, c % 2, q, :], ps_h[:, c % 2, q * FEAT:(q + 1) * FEAT],
                                                ACT.Copy, scale=cut_sb[:, ds(group(i, c) * TILES_PER_GROUP + q, 1)])
                last.then_inc(hcut_done, 1)

            def copy_merged(i, c):
                if not exists(i, c):
                    return
                act.wait_ge(gap_done, group(i, c) + 1)
                back = c - MERGED_SLOTS
                for q in range(TILES_PER_GROUP):
                    if exists(i, back):
                        act.wait_ge(added[chain(i, back, q)], (chain_scatters(i, back, q) + 1) * 16)
                nc.scalar.copy(
                    merged[:, c % MERGED_SLOTS, :, :].rearrange("p (a b) f -> p a b f", a=2),
                    ps_m[:, :, 0:2 * M].rearrange("p a (b m) -> p a b m", m=M)[:, :, :, 0:FEAT]).then_inc(copied, 1)

            def edge_step(i, c):
                clear_step(i, c)
                abs_step(i, c + 1)
                exp_step(i, c + 1)
                ln_step(i, c + 1)
                copy_merged(i, c - 1)
                cut_step(i, c + 1)
            over_edges(act, edge_step, 1, 1)

            def copy_agg(i, c):
                if not there(i, c):
                    return
                b, slot = i * NODE_SLOTS + c, c % 2
                act.wait_ge(aggt_mm, b + 1)
                if needed(b - 1):
                    act.wait_ge(z2_done, b - 1)
                nc.scalar.copy(agg_t[:, slot, :], ps_z[:, slot, :]).then_inc(aggt_done, 1)

            def out_ssp(i, c):
                if not there(i, c):
                    return
                b, slot = i * NODE_SLOTS + c, c % 2
                act.wait_ge(z2_done, b + 1)
                nc.scalar.activation(az[:, slot, :], ps_w[:, slot, :], ACT.Abs).then_inc(az2_done, 1)
                act.wait_ge(az2_done, b + 1)
                nc.scalar.activation(ez[:, slot, :], az[:, slot, :], ACT.Exp, scale=-1.0).then_inc(ez2_done, 1)
                act.wait_ge(ez2_done, b + 1)
                if needed(b - 1):
                    act.wait_ge(ssp2_done, b - 1)
                nc.scalar.activation(yz[:, slot, :], ez[:, slot, :], ACT.Ln, bias=half_sb[:, 0:1],
                                     scale=0.5).then_inc(y2_done, 1)

            def rstd_guess(i, c):
                if not there(i, c):
                    return
                b, slot = i * NODE_SLOTS + c, c % NODE_SLOTS
                act.wait_ge(stat_done, b + 1)
                nc.scalar.activation(rstd[:, slot, 0, :], mean_var[:, slot, :, 1], ACT.Ln,
                                     bias=eps_sb[:, 0:1]).then_inc(ln_done, 1)
                act.wait_ge(ln_done, b + 1)
                if needed(b - NODE_SLOTS + 1):
                    act.wait_ge(shift_done, b - NODE_SLOTS + 1)
                nc.scalar.activation(rstd[:, slot, 1, :], rstd[:, slot, 0, :], ACT.Exp, scale=-0.5).then_inc(r0_done, 1)

            def normalise(i, c):
                if not there(i, c):
                    return
                b, slot = i * NODE_SLOTS + c, c % NODE_SLOTS
                act.wait_ge(shift_done, b + 1)
                if needed(b - NODE_SLOTS + 1):
                    act.wait_ge(out_stored[slot], slot_dmas(i, c) - 16)
                for k in range(4):
                    last = nc.scalar.activation(y_out[:, slot, k, :], res[:, slot, k, :], ACT.Identity,
                                                bias=rstd[:, slot, 4, k:k + 1], scale=rstd[:, slot, 3, k:k + 1])
                last.then_inc(norm_done, 1)

            def out_step(i, c):
                copy_agg(i, c)
                rstd_guess(i, c - 4)
                out_ssp(i, c - 1)
                normalise(i, c - 5)
            over_batches(act, out_step, lag=5)

        @block.vector
        def _(dve):
            nc.vector.memset(ones16[:, :], 1.0).then_inc(prep_done, 1)
            nc.vector.memset(half_sb[:, :], 0.5).then_inc(prep_done, 1)
            nc.vector.memset(eps_sb[:, :], EPS).then_inc(prep_done, 1)
            dve.wait_ge(row_in, 32)
            nc.vector.tensor_copy(row16[:, 0, :], row32[:, 0, :]).then_inc(idx_dve, 1)
            nc.vector.tensor_copy(row16[:, 1, :], row32[:, 1, :]).then_inc(idx_dve, 1)
            by_section = row32[:, 1, :].rearrange("p (a e) -> p a e", a=2)
            nc.vector.tensor_reduce(top_f[:, :], by_section, AX.X, ALU.max).then_inc(idx_dve, 1)
            nc.vector.tensor_reduce(base_f[:, :], by_section, AX.X, ALU.min).then_inc(idx_dve, 1)
            dve.wait_ge(idx_dve, 4)
            nc.vector.tensor_scalar(base_f[:, :], base_f[:, :], float(ROWS - P), None, ALU.min).then_inc(idx_dve, 1)
            dve.wait_ge(idx_dve, 5)
            nc.vector.tensor_tensor(span_f[:, :], top_f[:, :], base_f[:, :], ALU.subtract).then_inc(idx_dve, 1)
            dve.wait_ge(bias_in, 16 * 3)
            whole, rest = bias_row, bias_rest
            nc.vector.tensor_copy(bias_part[:, 0, :], whole).then_inc(bias_dve, 1)
            dve.wait_ge(bias_dve, 1)
            nc.vector.tensor_tensor(rest, whole, bias_part[:, 0, :], ALU.subtract).then_inc(bias_dve, 1)
            dve.wait_ge(bias_dve, 2)
            nc.vector.tensor_copy(bias_part[:, 1, :], rest).then_inc(bias_dve, 1)
            dve.wait_ge(bias_dve, 3)
            nc.vector.tensor_tensor(bias_part[:, 2, :], rest, bias_part[:, 1, :], ALU.subtract).then_inc(bias_dve, 1)
            dve.wait_ge(bias_dve, 4)

            def h_rest_1(i, c):
                if not there(i, c):
                    return
                b, slot = i * NODE_SLOTS + c, c % NODE_SLOTS
                dve.wait_ge(h_hi, b + 1)
                nc.vector.tensor_tensor(h_rest[:, slot, :, :], ps_hx[slot].rearrange("p (k f) -> p k f", k=4),
                                        h_out[:, slot, :, 0, :], ALU.subtract).then_inc(h_r1, 1)

            def h_rest_2(i, c):
                if not there(i, c):
                    return
                b, slot = i * NODE_SLOTS + c, c % NODE_SLOTS
                dve.wait_ge(h_mid, b + 1)
                nc.vector.tensor_tensor(h_out[:, slot, :, 2, :], h_rest[:, slot, :, :], h_out[:, slot, :, 1, :],
                                        ALU.subtract).then_inc(h_lo, 1)

            def h_step(i, c):
                h_rest_1(i, c)
                h_rest_2(i, c - 1)
            over_batches(dve, h_step, lag=1)

            dve.wait_ge(const_in, 16 * CONST_DMAS)
            dve.wait_ge(col_in, 16 * COL_DMAS)
            nc.vector.tensor_copy(eye16[:, :], eye_sb[:, :]).then_inc(prep_done, 1)
            nc.vector.tensor_copy(msg[:, :, :, FEAT].rearrange("p a b -> p (a b)"),
                                  lane_sb[:, 2:3].to_broadcast([P, 8])).then_inc(prep_done, 1)
            nc.vector.tensor_copy(src_f[:, :], src_raw[:, :]).then_inc(prep_done, 1)
            nc.vector.tensor_scalar(spare_gap[:, :], src_raw[:, :], -1.0, lane_sb[:, 3:4],
                                    ALU.mult, ALU.add).then_inc(prep_done, 1)
            dve.wait_ge(base_in, 32)
            nc.vector.tensor_copy(base_reg[:, :], base_lane[0:1, :]).then_inc(prep_done, 1)
            nc.vector.tensor_reduce(span_max[:, :], span_row[:, :], AX.X, ALU.max).then_inc(prep_done, 1)
            dve.wait_ge(prep_done, 9)
            nc.vector.tensor_scalar(base_lane[:, :], base_lane[:, :], lane_sb[:, 0:1], None,
                                    ALU.add).then_inc(prep_done, 1)
            nc.vector.tensor_scalar(wide_flag[:, :], span_max[:, :], float(P), None, ALU.is_ge).then_inc(prep_done, 1)
            dve.wait_ge(prep_done, PREP_STEPS)

            def pick_step(i, c):
                if not exists(i, c):
                    return
                half = c % 2
                if half == 0:
                    dve.wait_ge(dst_loaded[section_slot(c)], section_loads(i, c))
                if needed(group(i, c) - 1):
                    dve.wait_ge(hg_done, group(i, c) - 1)
                nc.vector.tensor_scalar(pick[:, c % 2, :], dst_rep[:, section_slot(c), half * GROUP:(half + 1) * GROUP],
                                        base_lane[:, ds(section(i, c), 1)], None, ALU.is_equal).then_inc(pick_done, 1)

            def same_step(i, c):
                if not exists(i, c):
                    return
                half = c % 2
                if half == 0:
                    dve.wait_ge(src_loaded[section_slot(c)], section_loads(i, c))
                if needed(group(i, c) - 1):
                    dve.wait_ge(merge_done, group(i, c) - 1)
                nc.vector.tensor_tensor(
                    same[:, c % 2, :].rearrange("p (q e) -> p q e", q=4),
                    src_rep[:, section_slot(c), half * GROUP:(half + 1) * GROUP].rearrange("p (q e) -> p q e", q=4),
                    src_f[:, ds(group(i, c) * 4, 4)].unsqueeze(2).to_broadcast([P, 4, P]),
                    ALU.is_equal).then_inc(same_done, 1)

            def ssp_step(i, c):
                if not exists(i, c):
                    return
                dve.wait_ge(y_done, group(i, c) + 1)
                if needed(group(i, c) - 1):
                    dve.wait_ge(w_done, group(i, c) - 1)
                nc.vector.scalar_tensor_tensor(out=act1[:, c % 2, :], in0=ps_z[:, c % 2, :], scalar=0.0,
                                               in1=yz[:, c % 2, :], op0=ALU.max, op1=ALU.add).then_inc(ssp_done, 1)

            def msg_step(i, c):
                if not exists(i, c):
                    return
                dve.wait_ge(w_done, group(i, c) + 1)
                dve.wait_ge(hcut_done, group(i, c) + 1)
                if needed(group(i, c) - 1):
                    dve.wait_ge(merge_done, group(i, c) - 1)
                nc.vector.tensor_tensor(msg[:, c % 2, :, 0:FEAT], ps_w[:, c % 2, :].rearrange("p (q f) -> p q f", q=4),
                                        h_cut[:, c % 2, :, :], ALU.mult).then_inc(msg_done, 1)

            def idx_step(i, c):
                if not exists(i, c):
                    return
                dve.wait_ge(merge_done, group(i, c) + 1)
                nc.vector.scalar_tensor_tensor(
                    out=gap[:, c % MERGED_SLOTS, :].rearrange("p (a b) -> p a b", a=2),
                    in0=ps_m[:, :, 0:2 * M].rearrange("p a (b m) -> p a b m", m=M)[:, :, :, FEAT],
                    scalar=lane_sb[:, 1:2],
                    in1=spare_gap[:, ds(group(i, c) * TILES_PER_GROUP, TILES_PER_GROUP)].rearrange(
                        "p (a b) -> p a b", a=2),
                    op0=ALU.is_ge, op1=ALU.mult).then_inc(gap_done, 1)
                dve.wait_ge(gap_done, group(i, c) + 1)
                back = c - MERGED_SLOTS
                for q in range(TILES_PER_GROUP):
                    if exists(i, back):
                        dve.wait_ge(added[chain(i, back, q)], (chain_scatters(i, back, q) + 1) * 16)
                nc.vector.tensor_tensor(row_idx[:, c % MERGED_SLOTS, :], gap[:, c % MERGED_SLOTS, :],
                                        src_f[:, ds(group(i, c) * TILES_PER_GROUP, TILES_PER_GROUP)],
                                        ALU.add).then_inc(idx_done, 1)

            def edge_step(i, c):
                pick_step(i, c + 2)
                same_step(i, c)
                msg_step(i, c)
                idx_step(i, c - 1)
                ssp_step(i, c + 1)
            over_edges(dve, edge_step, 2, 1)

            def sum_all(i, c):
                if not there(i, c):
                    return
                b, slot = i * NODE_SLOTS + c, c % 2
                dve.wait_ge(pair_sums, b + 1)
                if needed(b - 1):
                    dve.wait_ge(aggt_mm, b - 1)
                nc.vector.tensor_tensor(agg[:, slot, :, :].rearrange("p k f -> p (k f)"), acc_part[:, slot, 0, :],
                                        acc_part[:, slot, 1, :], ALU.add).then_inc(agg_done, 1)

            def out_ssp(i, c):
                if not there(i, c):
                    return
                b, slot = i * NODE_SLOTS + c, c % 2
                dve.wait_ge(y2_done, b + 1)
                if needed(b - 1):
                    dve.wait_ge(o_done, b - 1)
                nc.vector.scalar_tensor_tensor(out=act1[:, slot, :], in0=ps_w[:, slot, :], scalar=0.0,
                                               in1=yz[:, slot, :], op0=ALU.max, op1=ALU.add).then_inc(ssp2_done, 1)

            def residual(i, c):
                if not there(i, c):
                    return
                b, slot = i * NODE_SLOTS + c, c % NODE_SLOTS
                dve.wait_ge(o_done, b + 1)
                dve.wait_ge(res_loaded[slot], slot_dmas(i, c))
                if needed(b - NODE_SLOTS + 1):
                    dve.wait_ge(norm_done, b - NODE_SLOTS + 1)
                nc.vector.tensor_tensor(res[:, slot, :, :].rearrange("p k f -> p (k f)"), ps_h[:, c % 2, :],
                                        x_in[:, slot, :], ALU.add).then_inc(res_done, 1)
                dve.wait_ge(res_done, b + 1)
                for k in range(4):
                    last = nc.vector.bn_stats(stats[:, slot, k, :], res[:, slot, k, :])
                last.then_inc(var_done, 1)
                dve.wait_ge(var_done, b + 1)
                dve.nop(nofuse=True)
                for k in range(4):
                    last = nc.vector.bn_aggr(mean_var[:, slot, k, :], stats[:, slot, k, :])
                last.then_inc(stat_done, 1)

            def rstd_step(i, c):
                if not there(i, c):
                    return
                b, slot = i * NODE_SLOTS + c, c % NODE_SLOTS
                r = [rstd[:, slot, k, :] for k in range(5)]
                dve.wait_ge(r0_done, b + 1)
                nc.vector.tensor_tensor(r[2], r[1], r[1], ALU.mult).then_inc(newton, 1)
                dve.wait_ge(newton, b * 4 + 1)
                nc.vector.scalar_tensor_tensor(out=r[3], in0=mean_var[:, slot, :, 1], scalar=EPS, in1=r[2],
                                               op0=ALU.add, op1=ALU.mult).then_inc(newton, 1)
                dve.wait_ge(newton, b * 4 + 2)
                nc.vector.tensor_scalar(r[4], r[3], -0.5, 1.5, ALU.mult, ALU.add).then_inc(newton, 1)
                dve.wait_ge(newton, b * 4 + 3)
                nc.vector.tensor_tensor(r[3], r[1], r[4], ALU.mult).then_inc(newton, 1)
                dve.wait_ge(newton, b * 4 + 4)
                nc.vector.scalar_tensor_tensor(out=r[4], in0=mean_var[:, slot, :, 0], scalar=-1.0, in1=r[3],
                                               op0=ALU.mult, op1=ALU.mult).then_inc(shift_done, 1)

            def out_step(i, c):
                sum_all(i, c)
                out_ssp(i, c - 2)
                residual(i, c - 3)
                rstd_step(i, c - 4)
            over_batches(dve, out_step, lag=4)


def kernel(x, src, dst, edge_attr3_1x20, edge_weight1, L0_gnn_W_in, L0_gnn_W_f1, L0_gnn_b_f1, L0_gnn_W_f2,
           L0_gnn_b_f2, L0_gnn_W_o1, L0_gnn_b_o1, L0_gnn_W_o2, L0_gnn_b_o2):
    import concourse.bacc as bacc
    from concourse.bass_utils import run_bass_kernel_spmd

    x, src, dst = np.asarray(x), np.asarray(src), np.asarray(dst)
    more_edges, more_rows = EDGE_ROWS - EDGES, ROWS - ATOMS
    x_rows = np.concatenate([x, np.zeros((more_rows, FEAT), x.dtype)])
    src_all = np.concatenate([src, np.full(more_edges, SPARE, src.dtype)])
    dst_all = np.concatenate([dst, np.full(more_edges, ATOMS - 1, dst.dtype)])
    cut = np.asarray(edge_weight1).reshape(EDGES)
    cut_all = np.concatenate([cut, np.zeros(more_edges, cut.dtype)])
    rbf = np.asarray(edge_attr3_1x20).reshape(EDGES, RBF)
    rbf_t = np.concatenate([np.concatenate([rbf.T, np.zeros((RBF, more_edges), rbf.dtype)], 1),
                            np.ones((1, EDGE_ROWS), rbf.dtype)])
    p = np.arange(P)
    lane = np.stack([p, 2.5 * 2.0 ** (60 - p), 2.0 ** (60 - p), SPARE + p], 1).astype(np.float32)

    def columns(v):
        return np.ascontiguousarray(v.reshape(TILES, P).T)

    arrays = {
        "x_rows": x_rows,
        "x_cols": np.ascontiguousarray(x_rows.reshape(BATCHES, P, 4, FEAT).transpose(3, 0, 2, 1).reshape(FEAT, ROWS)),
        "src_row": src_all.reshape(SECTIONS // 2, 2 * SECTION), "dst_row": dst_all.reshape(SECTIONS // 2, 2 * SECTION),
        "src_col": columns(src_all), "dst_col": columns(dst_all), "cut_col": columns(cut_all),
        "rbf_t": rbf_t,
        "w_in": np.asarray(L0_gnn_W_in), "w_f1": np.asarray(L0_gnn_W_f1),
        "b_f1": np.asarray(L0_gnn_b_f1).reshape(1, FEAT), "w_f2": np.asarray(L0_gnn_W_f2),
        "b_f2": np.asarray(L0_gnn_b_f2).reshape(1, FEAT), "w_o1": np.asarray(L0_gnn_W_o1),
        "b_o1": np.asarray(L0_gnn_b_o1).reshape(1, FEAT), "w_o2": np.asarray(L0_gnn_W_o2),
        "b_o2": np.asarray(L0_gnn_b_o2).reshape(1, FEAT),
        "lane": lane, "eye": np.eye(P, dtype=np.float32),
    }
    nc = bacc.Bacc("TRN2", target_bir_lowering=False, num_devices=1)
    args = [nc.dram_tensor(name, a.shape, mybir.dt.from_np(a.dtype), kind="ExternalInput").ap()
            for name, a in arrays.items()]
    out = nc.dram_tensor("out", (ATOMS, FEAT), mybir.dt.float32, kind="ExternalOutput").ap()
    gnn_program(nc, *args, out)
    result = run_bass_kernel_spmd(nc, [arrays], core_ids=[0])
    return result.results[0]["out"]
```
